# Optimizing a Trainium2 kernel written in Bass

```python
import numpy as np
import jax
import jax.numpy as jnp

def _softmax(x, axis=-1):
    return jax.nn.softmax(x, axis=axis)

def _gelu(x):
    return jax.nn.gelu(x, approximate=True)

def _silu(x):
    return jax.nn.silu(x)

def _sigmoid(x):
    return jax.nn.sigmoid(x)

def _layernorm(x, axis=-1, eps=1e-05):
    m = jnp.mean(x, axis=axis, keepdims=True)
    v = jnp.var(x, axis=axis, keepdims=True)
    return (x - m) / jnp.sqrt(v + eps)

def _scatter_add(tgt, idx, src, axis=0):
    return tgt.at[idx].add(src)

def _segment_sum(src, seg, n):
    return jax.ops.segment_sum(src, seg, n)
kernel_name = 'mk_xattn_ffn_d2_seqx_r4_bccd39'

def setup_inputs(seed: int=0):
    np.random.seed(seed)
    _w = jnp.asarray

    def _rec_inputs():
        import jax
        import jax.numpy as jnp
        _rk = jax.random.key(seed)
        x = -0.0002928 + 1 * jax.random.normal(jax.random.fold_in(_rk, 1), (16, 512, 256), jnp.float32)
        _lenS = 512 - jax.random.randint(jax.random.fold_in(_rk, 7), (16,), 0, max(1, 512 // 4) + 1, jnp.int32)
        _lenS2 = 1601 - jax.random.randint(jax.random.fold_in(_rk, 8), (16,), 0, max(1, 1601 // 4) + 1, jnp.int32)
        _ctx_1024P = jax.random.normal(jax.random.fold_in(_rk, 11), (16, 16, 256), jnp.float32)
        _ctx_1024c = jax.random.dirichlet(jax.random.fold_in(_rk, 511), 0.3 * jnp.ones((16,), jnp.float32), (16, 1601))
        _ctx_1024t = jnp.einsum('bsk,bkd->bsd', _ctx_1024c, _ctx_1024P)
        _ctx_1024t = _ctx_1024t * jax.lax.rsqrt(jnp.mean(jnp.square(_ctx_1024t)) + 1e-12) * 0.953939
        ctx_1024 = -1.39393e-06 + 0.999914 * (_ctx_1024t + 0.3 * jax.random.normal(jax.random.fold_in(_rk, 611), (16, 1601, 256), jnp.float32))
        _validS = jnp.arange(512)[None, :] < _lenS[:, None]
        _validS2 = jnp.arange(1601)[None, :] < _lenS2[:, None]
        _causal = jnp.tril(jnp.ones((512, 512), dtype=bool))
        mask_BxS2_bk0 = jnp.logical_not(jnp.broadcast_to(_validS2[:, :], (16, 1601)))
        return (x, ctx_1024, mask_BxS2_bk0)
    x, ctx_1024, mask_BxS2_bk0 = _rec_inputs()

    def _L0_xattn_setup():
        import jax, jax.numpy as jnp
        import numpy as np
        NUM_HEADS = 16
        D_MODEL = 256
        HEAD_DIM = D_MODEL // NUM_HEADS
        SCALE = float(np.sqrt(HEAD_DIM))
        EPS = 1e-05

        def layernorm(x, g, b):
            mu = jnp.mean(x, axis=-1, keepdims=True)
            var = jnp.mean(jnp.square(x - mu), axis=-1, keepdims=True)
            return (x - mu) * jax.lax.rsqrt(var + EPS) * g + b
        key = jax.random.key(seed)
        ks = jax.random.split(key, 8)
        B, Nq, Nc = (2, 512, 512)
        s = 0.02
        return {'x_query': jax.random.normal(ks[0], (B, Nq, D_MODEL), jnp.float32), 'x_context': jax.random.normal(ks[1], (B, Nc, D_MODEL), jnp.float32), 'Wq': jax.random.normal(ks[2], (D_MODEL, D_MODEL), jnp.float32) * s, 'Wkv': jax.random.normal(ks[3], (D_MODEL, 2 * D_MODEL), jnp.float32) * s, 'Wp': jax.random.normal(ks[4], (D_MODEL, D_MODEL), jnp.float32) * s, 'bp': jnp.zeros((D_MODEL,), jnp.float32), 'ln_g': jnp.ones((HEAD_DIM,), jnp.float32), 'ln_b': jnp.zeros((HEAD_DIM,), jnp.float32)}
    _L0_xattn_all = _L0_xattn_setup()
    _L0_xattn_in = {k: v for k, v in _L0_xattn_all.items() if k in ('Wq', 'Wkv', 'Wp', 'bp', 'ln_g', 'ln_b')}
    del _L0_xattn_all

    def _L0_ffn_setup():
        import jax, jax.numpy as jnp
        import numpy as np
        D_MODEL, D_FF, RANK = (256, 1024, 64)
        B, S = (4, 1024)
        key = jax.random.key(seed)
        ks = jax.random.split(key, 7)
        return {'x': jax.random.normal(ks[0], (B, S, D_MODEL), dtype=jnp.float32), 'U1': jax.random.normal(ks[1], (D_MODEL, RANK), dtype=jnp.float32) * 0.02, 'V1': jax.random.normal(ks[2], (RANK, D_FF), dtype=jnp.float32) * 0.02, 'b1': jnp.zeros((D_FF,), dtype=jnp.float32), 'U2': jax.random.normal(ks[3], (D_FF, RANK), dtype=jnp.float32) * 0.02, 'V2': jax.random.normal(ks[4], (RANK, D_MODEL), dtype=jnp.float32) * 0.02, 'b2': jnp.zeros((D_MODEL,), dtype=jnp.float32)}
    _L0_ffn_all = _L0_ffn_setup()
    _L0_ffn_in = {k: v for k, v in _L0_ffn_all.items() if k in ('U1', 'V1', 'b1', 'U2', 'V2', 'b2')}
    del _L0_ffn_all

    def _L1_xattn_setup():
        import math
        import jax, jax.numpy as jnp
        import numpy as np
        HIDDEN = 256
        NUM_HEADS = 16
        HEAD_DIM = HIDDEN // NUM_HEADS
        B, S = (4, 512)

        def _layer_norm_scores(x, eps=1e-08):
            mean = jnp.mean(x, axis=-1, keepdims=True)
            sigma = jnp.std(x, axis=-1, keepdims=True, ddof=1)
            return (x - mean) / (sigma + eps)
        key = jax.random.key(seed)
        ks = jax.random.split(key, 10)
        sc_in = 1.0 / math.sqrt(HIDDEN)
        inp = {'query': jax.random.normal(ks[0], (B, S, HIDDEN), jnp.float32), 'key': jax.random.normal(ks[1], (B, S, HIDDEN), jnp.float32), 'value': jax.random.normal(ks[2], (B, S, HIDDEN), jnp.float32), 'mask': jax.random.randint(ks[3], (B, S), 0, 2).astype(bool), 'Wq': jax.random.normal(ks[4], (HIDDEN, HEAD_DIM), jnp.float32) * sc_in, 'bq': jnp.zeros((HEAD_DIM,), jnp.float32), 'Wk': jax.random.normal(ks[5], (HIDDEN, HEAD_DIM), jnp.float32) * sc_in, 'bk': jnp.zeros((HEAD_DIM,), jnp.float32), 'Wv': jax.random.normal(ks[6], (HIDDEN, HEAD_DIM), jnp.float32) * sc_in, 'bv': jnp.zeros((HEAD_DIM,), jnp.float32), 'Wout': jax.random.normal(ks[7], (HIDDEN, HIDDEN), jnp.float32) * sc_in, 'bout': jnp.zeros((HIDDEN,), jnp.float32), 'seq_mask': 0}
        return inp
    _L1_xattn_all = _L1_xattn_setup()
    _L1_xattn_in = {k: v for k, v in _L1_xattn_all.items() if k in ('Wq', 'bq', 'Wk', 'bk', 'Wv', 'bv', 'Wout', 'bout')}
    del _L1_xattn_all

    def _L1_ffn_setup():
        import jax, jax.numpy as jnp
        import numpy as np
        B, M, D = (4, 512, 256)
        N, P = (64, 32)
        key = jax.random.key(seed)
        k1, k2, k3, k4 = jax.random.split(key, 4)
        x = jax.random.normal(k1, (B, M, D), dtype=jnp.float32)
        phi = jax.random.normal(k2, (D, N, P), dtype=jnp.float32) * (1.0 / np.sqrt(D))
        W = jax.random.normal(k3, (N, D, D), dtype=jnp.float32) * (1.0 / np.sqrt(D))
        b = jax.random.normal(k4, (N, D), dtype=jnp.float32) * 0.01
        return {'x': x, 'phi': phi, 'W': W, 'b': b}
    _L1_ffn_all = _L1_ffn_setup()
    _L1_ffn_in = {k: v for k, v in _L1_ffn_all.items() if k in ('phi', 'W', 'b')}
    del _L1_ffn_all
    return {'x': x, 'ctx_1024': ctx_1024, 'mask_BxS2_bk0': mask_BxS2_bk0, 'L0_xattn_Wq': _L0_xattn_in['Wq'], 'L0_xattn_Wkv': _L0_xattn_in['Wkv'], 'L0_xattn_Wp': _L0_xattn_in['Wp'], 'L0_xattn_bp': _L0_xattn_in['bp'], 'L0_xattn_ln_g': _L0_xattn_in['ln_g'], 'L0_xattn_ln_b': _L0_xattn_in['ln_b'], 'L0_ffn_U1': _L0_ffn_in['U1'], 'L0_ffn_V1': _L0_ffn_in['V1'], 'L0_ffn_b1': _L0_ffn_in['b1'], 'L0_ffn_U2': _L0_ffn_in['U2'], 'L0_ffn_V2': _L0_ffn_in['V2'], 'L0_ffn_b2': _L0_ffn_in['b2'], 'L1_xattn_Wq': _L1_xattn_in['Wq'], 'L1_xattn_bq': _L1_xattn_in['bq'], 'L1_xattn_Wk': _L1_xattn_in['Wk'], 'L1_xattn_bk': _L1_xattn_in['bk'], 'L1_xattn_Wv': _L1_xattn_in['Wv'], 'L1_xattn_bv': _L1_xattn_in['bv'], 'L1_xattn_Wout': _L1_xattn_in['Wout'], 'L1_xattn_bout': _L1_xattn_in['bout'], 'L1_ffn_phi': _L1_ffn_in['phi'], 'L1_ffn_W': _L1_ffn_in['W'], 'L1_ffn_b': _L1_ffn_in['b']}

def reference(x, ctx_1024, mask_BxS2_bk0, L0_xattn_Wq, L0_xattn_Wkv, L0_xattn_Wp, L0_xattn_bp, L0_xattn_ln_g, L0_xattn_ln_b, L0_ffn_U1, L0_ffn_V1, L0_ffn_b1, L0_ffn_U2, L0_ffn_V2, L0_ffn_b2, L1_xattn_Wq, L1_xattn_bq, L1_xattn_Wk, L1_xattn_bk, L1_xattn_Wv, L1_xattn_bv, L1_xattn_Wout, L1_xattn_bout, L1_ffn_phi, L1_ffn_W, L1_ffn_b):
    import jax
    import jax.numpy as jnp

    def _L0_xattn_ref(x_query, x_context, Wq, Wkv, Wp, bp, ln_g, ln_b):
        import jax, jax.numpy as jnp
        import numpy as np
        NUM_HEADS = 16
        D_MODEL = 256
        HEAD_DIM = D_MODEL // NUM_HEADS
        SCALE = float(np.sqrt(HEAD_DIM))
        EPS = 1e-05

        def layernorm(x, g, b):
            mu = jnp.mean(x, axis=-1, keepdims=True)
            var = jnp.mean(jnp.square(x - mu), axis=-1, keepdims=True)
            return (x - mu) * jax.lax.rsqrt(var + EPS) * g + b
        B, Nq, _ = x_query.shape
        Nc = x_context.shape[1]
        H, D = (NUM_HEADS, HEAD_DIM)
        q = (x_query @ Wq).reshape(B, Nq, H, D).transpose(0, 2, 1, 3)
        kv = (x_context @ Wkv).reshape(B, Nc, 2, H, D)
        k = kv[:, :, 0].transpose(0, 2, 1, 3)
        v = kv[:, :, 1].transpose(0, 2, 1, 3)
        q = layernorm(q, ln_g, ln_b)
        k = layernorm(k, ln_g, ln_b)
        q = q * SCALE
        attn = jnp.einsum('bhqd,bhkd->bhqk', q, k)
        attn = jax.nn.softmax(attn, axis=-1)
        out = jnp.einsum('bhqk,bhkd->bhqd', attn, v)
        out = out.transpose(0, 2, 1, 3).reshape(B, Nq, H * D)
        return out @ Wp + bp

    def _L0_ffn_ref(x, U1, V1, b1, U2, V2, b2):
        import jax, jax.numpy as jnp
        import numpy as np
        D_MODEL, D_FF, RANK = (256, 1024, 64)
        B, S = (4, 1024)
        P = jnp.einsum('bsd,dr->bsr', x, U1)
        H = jax.nn.gelu(jnp.einsum('bsr,rf->bsf', P, V1) + b1)
        Q = jnp.einsum('bsf,fr->bsr', H, U2)
        return jnp.einsum('bsr,rd->bsd', Q, V2) + b2

    def _L1_xattn_ref(query, key, value, mask, Wq, bq, Wk, bk, Wv, bv, Wout, bout, seq_mask):
        import math
        import jax, jax.numpy as jnp
        import numpy as np
        HIDDEN = 256
        NUM_HEADS = 16
        HEAD_DIM = HIDDEN // NUM_HEADS
        B, S = (4, 512)

        def _layer_norm_scores(x, eps=1e-08):
            mean = jnp.mean(x, axis=-1, keepdims=True)
            sigma = jnp.std(x, axis=-1, keepdims=True, ddof=1)
            return (x - mean) / (sigma + eps)
        q = query @ Wq + bq
        k = key @ Wk + bk
        v = value @ Wv + bv
        scores = jnp.einsum('bqd,bkd->bqk', q, k) / math.sqrt(HIDDEN)
        scores = _layer_norm_scores(scores)
        m = jnp.broadcast_to(mask[:, None, :], scores.shape)
        if seq_mask:
            tri = jnp.triu(jnp.ones(scores.shape[-2:], bool), k=1)
            m = m | tri[None]
        scores = scores + jnp.where(m, jnp.float32(-1e-32), jnp.float32(0.0))
        attn = jax.nn.softmax(scores, axis=-1)
        head = jnp.einsum('bqk,bkd->bqd', attn, v)
        attention = jnp.tile(head, (1, 1, NUM_HEADS))
        return attention @ Wout + bout

    def _L1_ffn_ref(x, phi, W, b):
        import jax, jax.numpy as jnp
        import numpy as np
        B, M, D = (4, 512, 256)
        N, P = (64, 32)
        logits = jnp.einsum('bmd,dnp->bmnp', x, phi)
        dispatch = jax.nn.softmax(logits, axis=0)
        bsz, m, n, p = logits.shape
        combine = jax.nn.softmax(logits.reshape(bsz, m, n * p), axis=-1).reshape(bsz, m, n, p)
        slots = jnp.einsum('bmd,bmnp->bnpd', x, dispatch)
        y = jnp.einsum('bnpd,nde->bnpe', slots, W) + b[None, :, None, :]
        out = jnp.einsum('bnpd,bmnp->bmd', y, combine)
        return out
    x = x + _L0_xattn_ref(_layernorm(x, axis=-1), ctx_1024, L0_xattn_Wq, L0_xattn_Wkv, L0_xattn_Wp, L0_xattn_bp, L0_xattn_ln_g, L0_xattn_ln_b)
    x = x + _L0_ffn_ref(_layernorm(x, axis=-1), L0_ffn_U1, L0_ffn_V1, L0_ffn_b1, L0_ffn_U2, L0_ffn_V2, L0_ffn_b2)
    x = x + _L1_xattn_ref(_layernorm(x, axis=-1), ctx_1024, ctx_1024, mask_BxS2_bk0, L1_xattn_Wq, L1_xattn_bq, L1_xattn_Wk, L1_xattn_bk, L1_xattn_Wv, L1_xattn_bv, L1_xattn_Wout, L1_xattn_bout, 0)
    x = x + _L1_ffn_ref(_layernorm(x, axis=-1), L1_ffn_phi, L1_ffn_W, L1_ffn_b)
    return x

_drawn_inputs = setup_inputs


def setup_inputs(seed=0):
    import zlib

    import numpy as np

    out = dict(_drawn_inputs(seed))
    spreads = {'L0_xattn_bp': (0.0, 0.1),
     'L0_xattn_ln_g': (1.0, 0.537),
     'L0_xattn_ln_b': (0.0, 0.8),
     'L0_ffn_b1': (0.0, 0.8),
     'L0_ffn_b2': (0.0, 0.774),
     'L1_xattn_bq': (0.0, 2.0),
     'L1_xattn_bk': (0.0, 2.0),
     'L1_xattn_bv': (0.0, 0.63),
     'L1_xattn_bout': (0.0, 0.75)}
    factors = {'L0_ffn_U1': 8.0,
     'L0_ffn_V1': 8.0,
     'L0_ffn_U2': 5.612,
     'L0_ffn_V2': 6.657,
     'L1_ffn_b': 200.0,
     'L1_xattn_Wq': 3.997}
    for name, (base, spread) in spreads.items():
        noise = np.random.default_rng([zlib.crc32(name.encode()), seed]).standard_normal(out[name].shape)
        drawn = base * np.exp(spread * noise) if base else spread * noise
        out[name] = jnp.asarray(drawn.astype(out[name].dtype))
    for name, factor in factors.items():
        out[name] = (out[name] * factor).astype(out[name].dtype)
    return out
```

```python
from contextlib import ExitStack

import concourse.bass as bass
from concourse import mybir

ALU = mybir.AluOpType
ACT = mybir.ActivationFunctionType
AX = mybir.AxisListType
F32 = mybir.dt.float32
BF16 = mybir.dt.bfloat16
I32 = mybir.dt.int32

P = 128
B, S, D = 16, 512, 256
NK = 1601
QT = S // P
KC = -(-NK // P)
KL = NK - (KC - 1) * P
H, HD = 16, 16
HG = 4
G = H // HG
TT = KC + QT
NP = 6 * HD
NR = NP + 3
PW = -(-NK // 4)
RANK, FF = 64, 1024
FC = FF // P
A1 = 16
NS, SP_, NE = 2048, 32, 64
SC = 256
EPS = 1e-5


def key_rows(c):
    return P if c < KC - 1 else KL


def transpose_bank_uses():
    order = []
    stack = lambda g: [("stack", g, u) for u in range(10)]
    order += stack(0) + stack(1) + [("max", 0, u) for u in range(2)]
    for g in range(G):
        if g > 0:
            order.append(("out", g - 1, 0))
        if g + 2 < G:
            order += stack(g + 2)
        if g + 1 < G:
            order += [("max", g + 1, u) for u in range(2)]
    order.append(("out", G - 1, 0))
    return {use: n for n, use in enumerate(order)}


USE = transpose_bank_uses()
USES = len(USE)


def layers(nc, x, ctx_in, mask, w, x3_d, xn_d, xnT_d, y_d, out):
    with ExitStack() as keep:
        sbk = lambda name, shape, dt=F32: keep.enter_context(nc.sbuf_tensor(name, shape, dt))
        ident = sbk("ident", [P, P])
        bank = [keep.enter_context(nc.psum_tensor(f"bank{i}", [P, 512], F32)) for i in range(8)]
        stage_one(nc, x, ctx_in, mask, w, x3_d, xn_d, xnT_d, ident, bank)
        stage_two(nc, w, x3_d, xn_d, xnT_d, y_d, out, ident, bank)


def stage_one(nc, x, ctx_d, mask, w, x3_d, xn_d, xnT_d, ident, bank_):
    with ExitStack() as st:
        sb = lambda name, shape, dt=F32: st.enter_context(nc.sbuf_tensor(name, shape, dt))
        sem = lambda name: st.enter_context(nc.semaphore(name))
        bank = [t[:, :] for t in bank_]

        identb = sb("identb", [P, P], BF16)
        wq = sb("wq", [P, 2, D])
        wkv = sb("wkv", [P, 2, 2 * D])
        wp = sb("wp", [P, 2, D])
        u1 = sb("u1", [P, 2, RANK])
        v1 = sb("v1", [RANK, FF])
        u2 = sb("u2", [P, FC, RANK])
        v2 = sb("v2", [RANK, D])
        b1c = sb("b1c", [P, FC])
        w1q = sb("w1q", [P, 2, A1])
        w1kv = sb("w1kv", [P, 2, 2 * A1])
        bq = sb("bq", [A1, 1])
        bkv = sb("bkv", [2 * A1, 1])
        wst = sb("wst", [P, D + 1])
        bpr = sb("bpr", [P, D])
        b2r = sb("b2r", [P, D])
        bor = sb("bor", [P, D])
        lng = sb("lng", [P, HD])
        lnb = sb("lnb", [P, HD])
        eps = sb("eps", [P, 1])
        mean_w = sb("mean_w", [P, 4, H])
        maskb = sb("maskb", [P, KC, B])

        ctx_sb = sb("ctx_sb", [P, KC, D])
        ctxT = sb("ctxT", [P, 2, KC * P])
        vaug = sb("vaug", [P, KC, H, HD + 1])
        kraw = sb("kraw", [P, TT, D])
        sq = sb("sq", [P, 4, D])
        ssq = sb("ssq", [P, TT, H])
        rstd = sb("rstd", [P, TT, H])
        kf = sb("kf", [P, TT, HG * HD])
        stack = [ctxT[:, :, :].rearrange("p a k -> p (a k)").bitcast(BF16)[:, 0:TT * HG * NP].rearrange(
            "p (t n) -> p t n", n=NP), sb("stack1", [P, TT * HG, NP], BF16)[:, :, :]]
        kst = [sb(f"kst{i}", [P, HG, KC * P], BF16) for i in range(3)]
        qst = [sb(f"qst{i}", [P, HG, S], BF16) for i in range(3)]
        mx = sb("mx", [P, HG * QT, 4])
        nmx = sb("nmx", [P, HG * QT])
        mxr = sb("mxr", [P, HG * QT])
        mxp = sb("mxp", [P, HG * QT, 4], BF16)
        probs = sb("probs", [P, 4, 1024])
        hT = probs[:, :, :].rearrange("p a b -> p (a b)").rearrange("p (f q) -> p f q", f=FC)
        o_sb = sb("o_sb", [P, S])
        rec = sb("rec", [P, QT * HG])
        attn = sb("attn", [P, QT, D])
        xin = sb("xin", [P, QT, D])
        xw = sb("xw", [P, QT, D])
        xv = sb("xv", [P, QT, D])
        xn = sb("xn", [P, QT, D])
        xnT = sb("xnT", [P, 2, S])
        bst = sb("bst", [P, QT, 6])
        mv = sb("mv", [P, QT, 2])
        std = sb("std", [P, QT])
        rs = sb("rs", [P, QT])
        pT = o_sb[0:RANK, :]
        kv1T = sb("kv1T", [2 * A1 + 1, NK])
        v1a = sb("v1a", [P, KC, 2 * A1])
        qa = sb("qa", [P, QT, 2 * A1 + 1])
        q1T = attn[0:A1, 0:2, :].rearrange("p a d -> p (a d)")
        q1a = attn[0:2 * A1 + 1, 2:4, :].rearrange("p a d -> p (a d)")
        st1 = sb("st1", [P, QT, 4, 6])
        mv1 = sb("mv1", [P, QT, 2])
        sg = sb("sg", [P, QT])
        maskcol = sb("maskcol", [P, KC])

        weights_in = sem("weights_in")
        ident_made = sem("ident_made")
        setup_dve = sem("setup_dve")
        setup_pool = sem("setup_pool")
        setup_pe = sem("setup_pe")
        ctx_loaded = sem("ctx_loaded")
        x_loaded = sem("x_loaded")
        x_based = sem("x_based")
        ln_var = sem("ln_var")
        ln_std = sem("ln_std")
        xn_ready = sem("xn_ready")
        xnT_mm = sem("xnT_mm")
        xnT_ready = sem("xnT_ready")
        q_mm = sem("q_mm")
        q_raw = sem("q_raw")
        ctx_tr = sem("ctx_tr")
        ctxT_ready = sem("ctxT_ready")
        kv_mm = sem("kv_mm")
        kv_raw = sem("kv_raw")
        sq_summed = sem("sq_summed")
        head_std = sem("head_std")
        head_rstd = sem("head_rstd")
        kv1_mm = sem("kv1_mm")
        kv1_ready = sem("kv1_ready")
        v1_tr = sem("v1_tr")
        v1_ready = sem("v1_ready")
        pool_step = sem("pool_step")
        kf_ready = sem("kf_ready")
        stack_ready = sem("stack_ready")
        t_full = sem("t_full")
        t_free = sem("t_free")
        m_full = sem("m_full")
        m_free = sem("m_free")
        mx_ready = sem("mx_ready")
        s_full = sem("s_full")
        s_exp = sem("s_exp")
        pv_mm = sem("pv_mm")
        o_copied = sem("o_copied")
        attn_tr = sem("attn_tr")
        attnT_ready = sem("attnT_ready")
        proj_mm = sem("proj_mm")
        x_new = sem("x_new")
        ffn_mm = sem("ffn_mm")
        ffn_act = sem("ffn_act")
        h_mm = sem("h_mm")
        h_act = sem("h_act")
        q1_mm = sem("q1_mm")
        q1_act = sem("q1_act")
        sc_mm = sem("sc_mm")
        sc_stat = sem("sc_stat")
        sc_var = sem("sc_var")
        sc_std = sem("sc_std")
        q1_tr = sem("q1_tr")
        qa_ready = sem("qa_ready")
        s1_mm = sem("s1_mm")
        s1_exp = sem("s1_exp")
        pv1_mm = sem("pv1_mm")
        o_copied_1 = sem("o_copied_1")
        dve_step = sem("dve_step")
        stored = sem("stored")

        DVE_STEPS = DVE_STEPS_PER_BATCH
        POOL_STEPS = 2 * G
        NW = 32

        block = st.enter_context(nc.Block())

        @block.sync
        def _(sp):
            loads = [
                (wq[:, :, :], w["L0_xattn_Wq"].rearrange("(k p) n -> p k n", p=P)),
                (wkv[:, :, :], w["L0_xattn_Wkv"].rearrange("(k p) n -> p k n", p=P)),
                (wp[:, :, :], w["L0_xattn_Wp"].rearrange("(k p) n -> p k n", p=P)),
                (u1[:, :, :], w["L0_ffn_U1"].rearrange("(k p) n -> p k n", p=P)),
                (v1[:, :], w["L0_ffn_V1"]),
                (u2[:, :, :], w["L0_ffn_U2"].rearrange("(k p) n -> p k n", p=P)),
                (v2[:, :], w["L0_ffn_V2"]),
                (b1c[:, :], w["L0_ffn_b1"].rearrange("(k p) -> p k", p=P)),
                (w1q[:, :, :], w["L1_xattn_Wq"].rearrange("(k p) n -> p k n", p=P)),
                (w1kv[:, :, 0:A1], w["L1_xattn_Wk"].rearrange("(k p) n -> p k n", p=P)),
                (w1kv[:, :, A1:2 * A1], w["L1_xattn_Wv"].rearrange("(k p) n -> p k n", p=P)),
                (bq[:, :], w["L1_xattn_bq"].rearrange("(p a) -> p a", a=1)),
                (bkv[0:A1, :], w["L1_xattn_bk"].rearrange("(p a) -> p a", a=1)),
                (bkv[A1:2 * A1, :], w["L1_xattn_bv"].rearrange("(p a) -> p a", a=1)),
                (bpr[:, :], w["L0_xattn_bp"].partition_broadcast(P)),
                (b2r[:, :], w["L0_ffn_b2"].partition_broadcast(P)),
                (bor[:, :], w["L1_xattn_bout"].partition_broadcast(P)),
                (lng[:, :], w["L0_xattn_ln_g"].partition_broadcast(P)),
                (lnb[:, :], w["L0_xattn_ln_b"].partition_broadcast(P)),
            ]
            for j in range(4):
                loads.append((probs[32 * j:32 * j + A1, :, :].rearrange("p a b -> p (a b)").rearrange(
                    "p (h n) -> p h n", h=H), w["L1_xattn_Wout"].rearrange("(h p) n -> p h n", p=A1)))
            loads.append((kraw[0:B, 0:7, :].rearrange("p a b -> p (a b)").bitcast(I32)[:, 0:NK], mask))
            for dst, src in loads:
                sp.dma_start(dst, src, allow_slow_non_contiguous=True).then_inc(weights_in, 16)
            assert len(loads) <= NW
            sp.wait_ge(weights_in, 16 * len(loads))
            sp.wait_ge(setup_dve, SETUP_DVE)
            sp.wait_ge(setup_pool, 4)
            with sp.Fori(0, B) as b:
                sp.wait_ge(ctxT_ready, 1 + b * KC)
                sp.dma_start(ctx_sb[:, 0:KC - 1, :],
                             ctx_d[b, 0:(KC - 1) * P, :].rearrange("(c p) d -> p c d", p=P)).then_inc(ctx_loaded, 16)
                sp.dma_start(ctx_sb[0:KL, KC - 1, :], ctx_d[b, (KC - 1) * P:NK, :]).then_inc(ctx_loaded, 16)
                sp.wait_ge(x_based, 1 + b * 3)
                sp.dma_start(xin[:, :, :], x[b].rearrange("(t p) d -> p t d", p=P)).then_inc(x_loaded, 16)
            sp.wait_ge(stored, 1 + 48 * B)

        NLOAD = 19 + 4 + 1

        @block.gpsimd
        def _(pool):
            pool.memset(ident[:, :], 0.0).then_inc(ident_made, 1)
            pool.wait_ge(ident_made, 1)
            pool.affine_select(out=ident[:, :], in_=ident[:, :], compare_op=ALU.not_equal, fill=1.0,
                               base=0, pattern=[[-1, P]], channel_multiplier=1).then_inc(ident_made, 1)
            pool.wait_ge(ident_made, 2)
            pool.tensor_copy(identb[:, :], ident[:, :]).then_inc(ident_made, 1)
            pool.wait_ge(ident_made, 3)
            for i in range(3):
                pool.memset(kst[i][96:NR, :, :], 1.0).then_inc(setup_pool, 1)
                pool.wait_ge(setup_pool, i + 1)
            pool.memset(eps[:, :], EPS).then_inc(setup_pool, 1)
            pool.wait_ge(setup_pool, 4)
            pool.sem_inc(x_based, 1)
            with pool.Fori(0, B) as b:
                pool.wait_ge(x_loaded, b * 16 + 16)
                pool.wait_ge(stored, 1 + b * 48)
                pool.tensor_tensor(xw[:, :, :], xin[:, :, :],
                                   bpr[:, None, :].broadcast_to((P, QT, D)), ALU.add).then_inc(x_based, 1)
                for g in range(G):
                    pool.wait_ge(head_rstd, b * 1 + 1)
                    if g >= 1:
                        pool.wait_ge(stack_ready, b * G + g)
                    hs = slice(HG * g, HG * g + HG)
                    kin = kraw[:, :, HG * HD * g:HG * HD * (g + 1)].rearrange("p t (h d) -> p t h d", h=HG)
                    kfv = kf[:, :, :].rearrange("p t (h d) -> p t h d", h=HG)
                    pool.tensor_tensor(kfv, kin, rstd[:, :, hs, None].broadcast_to((P, TT, HG, HD)),
                                       ALU.mult).then_inc(pool_step, 1)
                    pool.wait_ge(pool_step, b * POOL_STEPS + 2 * g + 1)
                    kf3 = kf[:, :, :].rearrange("p t (h d) -> p (t h) d", h=HG)
                    pool.tensor_tensor(kf3, kf3, lng[:, None, :].broadcast_to((P, TT * HG, HD)),
                                       ALU.mult).then_inc(pool_step, 1)
                    pool.wait_ge(pool_step, b * POOL_STEPS + 2 * g + 2)
                    pool.tensor_tensor(kf3, kf3, lnb[:, None, :].broadcast_to((P, TT * HG, HD)),
                                       ALU.add).then_inc(kf_ready, 1)
                pool.wait_ge(x_new, b * 3 + 1)
                pool.tensor_tensor(xv[:, :, :], xw[:, :, :],
                                   b2r[:, None, :].broadcast_to((P, QT, D)), ALU.add).then_inc(x_based, 1)
                pool.wait_ge(x_new, b * 3 + 2)
                pool.tensor_tensor(xw[:, :, :], xv[:, :, :],
                                   bor[:, None, :].broadcast_to((P, QT, D)), ALU.add).then_inc(x_based, 1)
            pool.wait_ge(stored, 1 + 48 * B)

        @block.tensor
        def _(pe):
            mm = nc.tensor.matmul
            tr = nc.tensor.transpose
            pe.wait_ge(ident_made, 3)
            pe.wait_ge(setup_dve, SETUP_DVE)
            pe.wait_ge(setup_pool, 4)
            for c in range(KC):
                m = key_rows(c)
                last = tr(bank[0][0:m, B * c:B * c + B], ctxT[0:B, 0, c * P:c * P + m], ident[0:B, 0:B])
            last.then_inc(setup_pe, 1)
            pe.wait_ge(setup_dve, SETUP_DVE + 1)

            with pe.Fori(0, B) as b:
                def transpose_x(k):
                    pe.wait_ge(xn_ready, b * 4 + k + 1)
                    for h in range(2):
                        for t in range(QT):
                            last = tr(bank[h][:, t * P:(t + 1) * P], xn[:, t, h * P:(h + 1) * P], ident[:, :])
                    last.then_inc(xnT_mm, 1)
                    pe.wait_ge(xnT_ready, 1 + b * 4 + k + 1)

                pe.wait_ge(xnT_ready, 1 + b * 4)
                transpose_x(0)
                for t in range(QT):
                    for k in range(2):
                        last = mm(bank[2 + t // 2][:, (t % 2) * D:(t % 2 + 1) * D], xnT[:, k, t * P:(t + 1) * P],
                                  wq[:, k, :], start=(k == 0), stop=(k == 1))
                last.then_inc(q_mm, 1)

                def transpose_ctx(c):
                    m = key_rows(c)
                    if c == 0:
                        pe.wait_ge(ctx_loaded, b * 32 + 32)
                    if c >= 2:
                        pe.wait_ge(ctxT_ready, 1 + b * KC + c - 1)
                    for h in range(2):
                        last = tr(bank[c % 2][:, h * P:h * P + m], ctx_sb[0:m, c, h * P:(h + 1) * P],
                                  ident[0:m, 0:m])
                    last.then_inc(ctx_tr, 1)

                def keys_values(c):
                    m = key_rows(c)
                    pe.wait_ge(ctxT_ready, 1 + b * KC + c + 1)
                    if c >= 4:
                        pe.wait_ge(kv_raw, b * KC + c - 3)
                    for k in range(2):
                        last = mm(bank[4 + c % 4][0:m, :], ctxT[:, k, c * P:c * P + m], wkv[:, k, :],
                                  start=(k == 0), stop=(k == 1))
                    last.then_inc(kv_mm, 1)

                transpose_ctx(0)
                for c in range(KC):
                    if c + 1 < KC:
                        transpose_ctx(c + 1)
                    keys_values(c)
                for i in range(4):
                    n = min(PW, NK - i * PW)
                    if i < 2:
                        pe.wait_ge(q_raw, b + 1)
                    else:
                        pe.wait_ge(kv1_ready, b * 4 + i - 1)
                    for k in range(2):
                        last = mm(bank[2 + i % 2][0:2 * A1, 0:n], w1kv[:, k, :], ctxT[:, k, i * PW:i * PW + n],
                                  start=(k == 0), stop=(k == 1))
                    last.then_inc(kv1_mm, 1)
                pe.wait_ge(kv1_ready, b * 4 + 4)
                tr(bank[1][:, 0:P], ident[:, :], ident[:, :])
                for c in range(KC):
                    m = key_rows(c)
                    last = tr(bank[0][0:m, 32 * c:32 * c + 32], kv1T[0:32, c * P:c * P + m], ident[0:32, 0:32])
                last.then_inc(v1_tr, 1)
                pe.wait_ge(kv_raw, b * KC + KC)

                tb = bank[6].bitcast(BF16)

                def stack_unit(g, u):
                    n = USE["stack", g, u]
                    if u == 0:
                        pe.wait_ge(stack_ready, b * G + g + 1)
                    pe.wait_ge(t_free, b * USES + n)
                    j, half = u // 2, u % 2
                    if u < 8:
                        tiles = [(t, j) for t in (range(8) if half == 0 else range(8, KC))]
                    else:
                        tiles = [(KC + t, 2 * (u - 8) + a) for a in range(2) for t in range(QT)]
                    for i, (t, hj) in enumerate(tiles):
                        m = KL if t == KC - 1 else P
                        last = tr(tb[0:NP, i * P:i * P + m], stack[g % 2][0:m, t * HG + hj, :], identb[0:m, 0:m])
                    last.then_inc(t_full, 1)

                def max_unit(g, u):
                    n = USE["max", g, u]
                    if u == 0:
                        pe.wait_ge(mx_ready, b * G + g + 1)
                    pe.wait_ge(t_free, b * USES + n)
                    for i in range(2 * QT):
                        last = tr(tb[96:NR, i * P:(i + 1) * P], mxp[:, 2 * QT * u + i, 0:3], identb[:, :])
                    last.then_inc(t_full, 1)

                def out_unit(g):
                    n = USE["out", g, 0]
                    pe.wait_ge(o_copied, b * G + g + 1)
                    pe.wait_ge(t_free, b * USES + n)
                    for t in range(QT):
                        last = tr(bank[6][:, t * P:(t + 1) * P], o_sb[:, t * P:(t + 1) * P], ident[:, :])
                    last.then_inc(t_full, 1)

                def score_rows(g, u):
                    n = 64 * g + u
                    j, t, i = u // 16, (u // 4) % 4, u % 4
                    if u == 0:
                        pe.wait_ge(t_free, b * USES + USE["stack", g, 9] + 1)
                    if n >= 2:
                        pe.wait_ge(m_free, b * 64 * G + n - 1)
                    k0 = min(i * PW, NK - PW)
                    mm(bank[4 + n % 2][:, 0:PW], qst[g % 3][0:NP, j, t * P:(t + 1) * P],
                       kst[g % 3][0:NP, j, k0:k0 + PW], start=True, stop=True).then_inc(m_full, 1)

                def score_cols(g, c):
                    m = key_rows(c)
                    for i in range(2):
                        n = 2 * (KC * g + c) + i
                        if n >= 2:
                            pe.wait_ge(s_exp, b * 2 * KC * G + n - 1)
                        for a in range(2):
                            j = 2 * i + a
                            last = mm(bank[2 * i + a][0:m, :], kst[g % 3][0:NR, j, c * P:c * P + m],
                                      qst[g % 3][0:NR, j, :], start=True, stop=True)
                        last.then_inc(s_full, 1)

                def weigh_values(g, c):
                    m = key_rows(c)
                    pe.wait_ge(s_exp, b * 2 * KC * G + 2 * (KC * g + c) + 2)
                    if c == 0 and g >= 1:
                        pe.wait_ge(o_copied, b * G + g)
                    for j in range(HG):
                        last = mm(bank[7][32 * j:32 * j + HD + 1, :], vaug[0:m, c, HG * g + j, :],
                                  probs[0:m, (2 * c + j // 2) % 4, (j % 2) * 512:(j % 2 + 1) * 512],
                                  start=(c == 0), stop=(c == KC - 1), skip_group_check=True)
                    last.then_inc(pv_mm, 1)

                for u in range(10):
                    stack_unit(0, u)
                for u in range(64):
                    score_rows(0, u)
                for u in range(10):
                    stack_unit(1, u)
                for u in range(2):
                    max_unit(0, u)
                for g in range(G):
                    pe.wait_ge(t_free, b * USES + USE["max", g, 1] + 1)
                    done = 0
                    for c in range(KC):
                        score_cols(g, c)
                        if c >= 1:
                            weigh_values(g, c - 1)
                        if c == 0 and g >= 1:
                            out_unit(g - 1)
                        if 2 <= c < 12 and g + 2 < G:
                            stack_unit(g + 2, c - 2)
                        if g + 1 < G:
                            until = 64 * (c + 1) // KC
                            for u in range(done, until):
                                score_rows(g + 1, u)
                            done = until
                    weigh_values(g, KC - 1)
                    if g + 1 < G:
                        for u in range(2):
                            max_unit(g + 1, u)
                out_unit(G - 1)

                pe.wait_ge(t_free, b * USES + USES)
                for h in range(2):
                    for t in range(QT):
                        last = tr(bank[h][:, t * P:(t + 1) * P], attn[:, t, h * P:(h + 1) * P], ident[:, :])
                last.then_inc(attn_tr, 1)
                pe.wait_ge(attnT_ready, b + 1)
                for t in range(QT):
                    for k in range(2):
                        last = mm(bank[2 + t // 2][:, (t % 2) * D:(t % 2 + 1) * D], xnT[:, k, t * P:(t + 1) * P],
                                  wp[:, k, :], start=(k == 0), stop=(k == 1))
                last.then_inc(proj_mm, 1)

                transpose_x(1)
                for k in range(2):
                    last = mm(bank[4][0:RANK, :], u1[:, k, :], xnT[:, k, :], start=(k == 0), stop=(k == 1))
                last.then_inc(ffn_mm, 1)
                pe.wait_ge(ffn_act, b * 2 + 1)
                for f in range(FC + 2):
                    if f < FC:
                        if f >= 2:
                            pe.wait_ge(h_act, b * FC + f - 1)
                        mm(bank[f % 2][:, :], v1[:, f * P:(f + 1) * P], pT, start=True, stop=True).then_inc(h_mm, 1)
                    if f >= 2:
                        pe.wait_ge(h_act, b * FC + f - 1)
                        last = mm(bank[5][0:RANK, :], u2[:, f - 2, :], hT[:, f - 2, :], start=(f == 2),
                                  stop=(f == FC + 1))
                last.then_inc(ffn_mm, 1)
                pe.wait_ge(ffn_act, b * 2 + 2)
                for t in range(QT):
                    last = mm(bank[2 + t // 2][:, (t % 2) * D:(t % 2 + 1) * D], pT[:, t * P:(t + 1) * P],
                              v2[:, :], start=True, stop=True)
                last.then_inc(proj_mm, 1)

                transpose_x(2)
                for k in range(2):
                    last = mm(bank[2][0:A1, :], w1q[:, k, :], xnT[:, k, :], start=(k == 0), stop=(k == 1))
                last.then_inc(q1_mm, 1)
                pe.wait_ge(q1_act, b + 1)
                for t in range(QT):
                    for i in range(4):
                        n = 4 * t + i
                        w_ = min(PW, NK - i * PW)
                        if n >= 4:
                            pe.wait_ge(sc_stat, b * 16 + n - 3)
                        mm(bank[4 + i][:, 0:w_], q1T[:, t * P:(t + 1) * P], kv1T[0:A1, i * PW:i * PW + w_],
                           start=True, stop=True).then_inc(sc_mm, 1)
                for t in range(QT):
                    last = tr(bank[2][:, t * A1:(t + 1) * A1], q1T[:, t * P:(t + 1) * P], ident[0:A1, 0:A1])
                last.then_inc(q1_tr, 1)
                pe.wait_ge(qa_ready, b * 2 + 1)
                tr(bank[1][:, 0:P], ident[:, :], ident[:, :])
                for t in range(QT):
                    last = tr(bank[3][0:2 * A1 + 1, t * P:(t + 1) * P], qa[:, t, :], ident[:, :])
                last.then_inc(q1_tr, 1)
                pe.wait_ge(qa_ready, b * 2 + 2)
                for c in range(KC + 2):
                    if c < KC:
                        m = key_rows(c)
                        if c >= 4:
                            pe.wait_ge(s1_exp, b * KC + c - 3)
                        mm(bank[4 + c % 4][0:m, :], kv1T[:, c * P:c * P + m], q1a[:, :], start=True,
                           stop=True).then_inc(s1_mm, 1)
                    if c >= 2:
                        e = c - 2
                        m = key_rows(e)
                        pe.wait_ge(s1_exp, b * KC + e + 1)
                        j = e % 4
                        last = mm(bank[0][32 * j:32 * j + 32, :], v1a[0:m, e, :],
                                  probs[0:m, j, (e // 4 % 2) * 512:(e // 4 % 2 + 1) * 512],
                                  start=(e < 4), stop=(e + 4 >= KC), skip_group_check=True)
                        last.then_inc(pv1_mm, 1)
                pe.wait_ge(o_copied_1, b + 1)
                for t in range(QT):
                    last = mm(bank[2 + t][:, 0:D + 1], o_sb[:, t * P:(t + 1) * P], wst[:, :], start=True, stop=True)
                last.then_inc(proj_mm, 1)
                transpose_x(3)

        @block.scalar
        def _(act):
            fn = nc.scalar.activation
            act.wait_ge(setup_dve, SETUP_DVE + 1)
            act.wait_ge(setup_pool, 4)
            act.sem_inc(stored, 1)
            with act.Fori(0, B) as b:
                def layer_norm_std(k):
                    act.wait_ge(ln_var, b * 4 + k + 1)
                    fn(std[:, :], mv[:, :, 1], ACT.Sqrt, bias=eps[:, 0:1]).then_inc(ln_std, 1)

                layer_norm_std(0)
                act.wait_ge(q_mm, b + 1)
                fn(kraw[:, KC:KC + 2, :].rearrange("p a d -> p (a d)"), bank[2], ACT.Copy)
                fn(kraw[:, KC + 2:KC + 4, :].rearrange("p a d -> p (a d)"), bank[3], ACT.Copy).then_inc(q_raw, 1)
                for c in range(KC):
                    m = key_rows(c)
                    act.wait_ge(kv_mm, b * KC + c + 1)
                    src = bank[4 + c % 4]
                    if c >= 4:
                        act.wait_ge(sq_summed, b * (KC + 1) + c - 3)
                    fn(sq[0:m, c % 4, :], src[0:m, 0:D], ACT.Square)
                    fn(vaug[0:m, c, :, 0:HD], src[0:m, D:2 * D].rearrange("p (h d) -> p h d", h=H), ACT.Copy)
                    fn(kraw[0:m, c, :], src[0:m, 0:D], ACT.Copy).then_inc(kv_raw, 1)
                for i in range(4):
                    n = min(PW, NK - i * PW)
                    act.wait_ge(kv1_mm, b * 4 + i + 1)
                    fn(kv1T[0:2 * A1, i * PW:i * PW + n], bank[2 + i % 2][0:2 * A1, 0:n], ACT.Identity,
                       bias=bkv[:, 0:1]).then_inc(kv1_ready, 1)
                act.wait_ge(sq_summed, b * (KC + 1) + KC + 1)
                fn(rstd[:, :, :], ssq[:, :, :], ACT.Sqrt, bias=eps[:, 0:1], scale=1.0 / HD).then_inc(head_std, 1)

                tb = bank[6].bitcast(BF16)

                def stack_evac(g, u):
                    act.wait_ge(t_full, b * USES + USE["stack", g, u] + 1)
                    if u < 8:
                        n = 8 * P if u % 2 == 0 else NK - 8 * P
                        dst = kst[g % 3][0:NP, u // 2, (u % 2) * 8 * P:(u % 2) * 8 * P + n]
                    else:
                        n = 2 * S
                        dst = qst[g % 3][0:NP, 2 * (u - 8):2 * (u - 8) + 2, :].rearrange("p a q -> p (a q)")
                    fn(dst, tb[0:NP, 0:n], ACT.Copy).then_inc(t_free, 1)

                def max_evac(g, u):
                    act.wait_ge(t_full, b * USES + USE["max", g, u] + 1)
                    fn(qst[g % 3][96:NR, 2 * u:2 * u + 2, :].rearrange("p a q -> p (a q)"), tb[96:NR, 0:2 * S],
                       ACT.Copy).then_inc(t_free, 1)

                for u in range(10):
                    stack_evac(0, u)
                for u in range(10):
                    stack_evac(1, u)
                for u in range(2):
                    max_evac(0, u)
                for g in range(G):
                    for c in range(KC):
                        m = key_rows(c)
                        for i in range(2):
                            act.wait_ge(s_full, b * 2 * KC * G + 2 * (KC * g + c) + i + 1)
                            if KC * g + c >= 2:
                                act.wait_ge(pv_mm, b * KC * G + KC * g + c - 1)
                            for a in range(2):
                                e = fn(probs[0:m, (2 * c + i) % 4, 512 * a:512 * a + 512], bank[2 * i + a][0:m, :],
                                       ACT.Exp, scale=float(HD) ** 0.5)
                            e.then_inc(s_exp, 1)
                        if 2 <= c < 12 and g + 2 < G:
                            stack_evac(g + 2, c - 2)
                    act.wait_ge(pv_mm, b * KC * G + KC * (g + 1))
                    if g >= 1:
                        act.wait_ge(t_full, b * USES + USE["out", g - 1, 0] + 1)
                    fn(o_sb[:, :], bank[7], ACT.Copy).then_inc(o_copied, 1)
                    if g + 1 < G:
                        for u in range(2):
                            max_evac(g + 1, u)

                layer_norm_std(1)
                act.wait_ge(ffn_mm, b * 2 + 1)
                act.wait_ge(t_full, b * USES + USES)
                fn(pT, bank[4][0:RANK, :], ACT.Copy).then_inc(ffn_act, 1)
                for f in range(FC):
                    act.wait_ge(h_mm, b * FC + f + 1)
                    fn(hT[:, f, :], bank[f % 2], ACT.Gelu_apprx_tanh, bias=b1c[:, f:f + 1]).then_inc(h_act, 1)
                act.wait_ge(ffn_mm, b * 2 + 2)
                fn(pT, bank[5][0:RANK, :], ACT.Copy).then_inc(ffn_act, 1)
                layer_norm_std(2)
                act.wait_ge(q1_mm, b + 1)
                fn(q1T[:, :], bank[2][0:A1, :], ACT.Identity, bias=bq[:, 0:1], scale=1.0 / A1).then_inc(q1_act, 1)
                act.wait_ge(sc_var, b + 1)
                fn(sg[:, :], mv1[:, :, 1], ACT.Sqrt, scale=NK / (NK - 1.0)).then_inc(sc_std, 1)
                for c in range(KC):
                    m = key_rows(c)
                    act.wait_ge(s1_mm, b * KC + c + 1)
                    if c >= 8:
                        act.wait_ge(pv1_mm, b * KC + c - 7)
                    fn(probs[0:m, c % 4, (c // 4 % 2) * 512:(c // 4 % 2 + 1) * 512], bank[4 + c % 4][0:m, :],
                       ACT.Exp, bias=maskcol[0:m, c:c + 1]).then_inc(s1_exp, 1)
                act.wait_ge(pv1_mm, b * KC + KC)
                fn(o_sb[:, :], bank[0], ACT.Copy).then_inc(o_copied_1, 1)
                layer_norm_std(3)
                act.wait_ge(x_new, b * 3 + 3)
                act.dma_start(x3_d[b].rearrange("(t p) d -> p t d", p=P), xw[:, :, :]).then_inc(stored, 16)
                act.wait_ge(xn_ready, b * 4 + 4)
                act.dma_start(xn_d[b].rearrange("(t p) d -> p t d", p=P), xn[:, :, :]).then_inc(stored, 16)
                act.wait_ge(xnT_ready, 1 + b * 4 + 4)
                act.dma_start(xnT_d[b], xnT[:, :, :]).then_inc(stored, 16)

        @block.vector
        def _(dve):
            v = nc.vector
            steps = [0]

            def setup(ins):
                steps[0] += 1
                ins.then_inc(setup_dve, 1)
                dve.wait_ge(setup_dve, steps[0])

            for i in range(8):
                setup(v.memset(bank[i], 0.0))
            setup(v.memset(vaug[:, :, :, HD:HD + 1], 1.0))
            setup(v.memset(ssq[:, :, :], 1.0))
            setup(v.memset(v1a[:, :, :], 0.0))
            setup(v.memset(v1a[:, :, A1:A1 + 1], 1.0))
            setup(v.memset(kv1T[2 * A1:2 * A1 + 1, :], 1.0))
            setup(v.memset(qa[:, :, :], 0.0))
            setup(v.memset(wst[:, :], 0.0))
            setup(v.memset(maskb[:, :, :], 0.0))
            setup(v.memset(mean_w[:, :, :], 0.0))
            dve.wait_ge(weights_in, 16 * NLOAD)
            setup(v.tensor_copy(ctxT[0:B, 0, 0:NK], kraw[0:B, 0:7, :].rearrange("p a b -> p (a b)").bitcast(I32)[:, 0:NK]))
            for k in range(2):
                for n, wt in ((k, wq[:, k, :]), (2 + k, wkv[:, k, 0:D])):
                    wh = wt.rearrange("p (h d) -> p h d", h=H)
                    setup(v.tensor_reduce(mean_w[:, n, :], wh, AX.X, ALU.add))
                    setup(v.tensor_scalar(mean_w[:, n, :], mean_w[:, n, :], 1.0 / HD, None, ALU.mult))
                    setup(v.tensor_tensor(wh, wh, mean_w[:, n, :, None].broadcast_to((P, H, HD)), ALU.subtract))
            for j in range(4):
                setup(v.tensor_reduce(wst[32 * j:32 * j + A1, 0:D],
                                      probs[32 * j:32 * j + A1, :, :].rearrange("p a b -> p (a b)").rearrange(
                                          "p (h n) -> p n h", h=H), AX.X, ALU.add))
            dve.wait_ge(ident_made, 3)
            for j in range(4):
                setup(v.tensor_copy(wst[32 * j:32 * j + 32, D:D + 1],
                                    ident[32 * j:32 * j + 32, 32 * j + A1:32 * j + A1 + 1]))
            setup(v.tensor_scalar(bq[:, :], bq[:, :], 1.0 / A1, None, ALU.mult))
            setup(v.memset(kraw[:, :, :], 0.0))
            assert steps[0] == SETUP_DVE, steps
            dve.wait_ge(setup_pe, 1)
            v.tensor_scalar(maskb[:, 0:KC - 1, :], bank[0][:, 0:(KC - 1) * B].rearrange("p (c b) -> p c b", b=B),
                            -1e-32, None, ALU.mult)
            v.tensor_scalar(maskb[0:KL, KC - 1, :], bank[0][0:KL, (KC - 1) * B:KC * B],
                            -1e-32, None, ALU.mult).then_inc(setup_dve, 1)
            dve.wait_ge(setup_dve, SETUP_DVE + 1)
            dve.sem_inc(ctxT_ready, 1)
            dve.sem_inc(xnT_ready, 1)
            with dve.Fori(0, B) as b:
                count = [0]

                def link(ins):
                    count[0] += 1
                    ins.then_inc(dve_step, 1)
                    dve.wait_ge(dve_step, b * DVE_STEPS + count[0])

                def layer_norm(k, src):
                    for t in range(QT):
                        ins = v.bn_stats(bst[:, t, :], src[:, t, :])
                    link(ins)
                    v.tensor_copy(rs[:, :], bst[:, :, 0])
                    for t in range(QT):
                        ins = v.bn_aggr(mv[:, t, :], bst[:, t, :])
                    ins.then_inc(ln_var, 1)
                    dve.wait_ge(ln_std, b * 4 + k + 1)
                    link(v.reciprocal(rs[:, :], std[:, :]))
                    for t in range(QT):
                        ins = v.tensor_scalar(xn[:, t, :], src[:, t, :], mv[:, t, 0:1], rs[:, t:t + 1],
                                              ALU.subtract, ALU.mult)
                    ins.then_inc(xn_ready, 1)

                def xT_copy(k):
                    dve.wait_ge(xnT_mm, b * 4 + k + 1)
                    v.tensor_copy(xnT[:, 0, :], bank[0])
                    v.tensor_copy(xnT[:, 1, :], bank[1]).then_inc(xnT_ready, 1)

                dve.wait_ge(x_loaded, b * 16 + 16)
                dve.wait_ge(stored, 1 + b * 48)
                link(v.tensor_copy(maskcol[:, :, None], maskb[:, :, bass.ds(b, 1)]))
                layer_norm(0, xin)
                xT_copy(0)
                for c in range(KC + 1):
                    if c < KC:
                        m = key_rows(c)
                        dve.wait_ge(ctx_tr, b * KC + c + 1)
                        v.tensor_copy(ctxT[:, :, c * P:c * P + m],
                                      bank[c % 2][:, 0:2 * P].rearrange("p (h k) -> p h k", h=2)[:, :, 0:m])\
                            .then_inc(ctxT_ready, 1)
                    if c >= 1:
                        m = key_rows(c - 1)
                        dve.wait_ge(kv_raw, b * KC + c)
                        v.tensor_reduce(ssq[0:m, c - 1, :], sq[0:m, (c - 1) % 4, :].rearrange("p (h d) -> p h d", h=H),
                                        AX.X, ALU.add).then_inc(sq_summed, 1)
                dve.wait_ge(q_raw, b + 1)
                dve.wait_ge(sq_summed, b * (KC + 1) + KC)
                qv = kraw[:, KC:TT, :]
                link(v.tensor_tensor(sq[:, :, :], qv, qv, ALU.mult))
                v.tensor_reduce(ssq[:, KC:TT, :], sq[:, :, :].rearrange("p t (h d) -> p t h d", h=H),
                                AX.X, ALU.add).then_inc(sq_summed, 1)
                dve.wait_ge(v1_tr, b + 1)
                bv = bank[0][:, 0:32 * KC].rearrange("p (c n) -> p c n", n=32)
                v.tensor_copy(v1a[:, 0:KC - 1, 0:A1], bv[:, 0:KC - 1, A1:2 * A1])
                v.tensor_copy(v1a[0:KL, KC - 1, 0:A1], bv[0:KL, KC - 1, A1:2 * A1]).then_inc(v1_ready, 1)
                dve.wait_ge(head_std, b + 1)
                v.reciprocal(rstd[:, :, :], rstd[:, :, :]).then_inc(head_rstd, 1)

                def split(g):
                    dve.wait_ge(kf_ready, b * G + g + 1)
                    if g >= 2:
                        dve.wait_ge(t_full, b * USES + USE["stack", g - 2, 9] + 1)
                    sk = stack[g % 2][:, 0:KC * HG, :].rearrange("p t (s d) -> p t s d", d=HD)
                    sqq = stack[g % 2][:, KC * HG:, :].rearrange("p t (s d) -> p t s d", d=HD)
                    kfk = kf[:, 0:KC, :].rearrange("p t (h d) -> p (t h) d", d=HD)
                    kfq = kf[:, KC:TT, :].rearrange("p t (h d) -> p (t h) d", d=HD)
                    NKH, NQH = KC * HG, QT * HG
                    v.tensor_copy(sk[:, :, 0:3, :], kfk[:, :, None, :].broadcast_to((P, NKH, 3, HD)))
                    v.tensor_copy(sqq[:, :, 3:6:2, :], kfq[:, :, None, :].broadcast_to((P, NQH, 2, HD)))
                    link(v.tensor_copy(sqq[:, :, 0, :], kfq))
                    v.tensor_tensor(kfk, kfk, sk[:, :, 0, :], ALU.subtract)
                    link(v.tensor_tensor(kfq, kfq, sqq[:, :, 0, :], ALU.subtract))
                    v.tensor_copy(sk[:, :, 3:5, :], kfk[:, :, None, :].broadcast_to((P, NKH, 2, HD)))
                    link(v.tensor_copy(sqq[:, :, 1:5:3, :], kfq[:, :, None, :].broadcast_to((P, NQH, 2, HD))))
                    v.tensor_tensor(sk[:, :, 5, :], kfk, sk[:, :, 3, :], ALU.subtract)
                    v.tensor_tensor(sqq[:, :, 2, :], kfq, sqq[:, :, 1, :], ALU.subtract).then_inc(stack_ready, 1)

                def row_maxima(g):
                    for u in range(64):
                        n = 64 * g + u
                        dve.wait_ge(m_full, b * 64 * G + n + 1)
                        v.tensor_reduce(mx[:, u // 4, u % 4:u % 4 + 1], bank[4 + n % 2][:, 0:PW], AX.X,
                                        ALU.max).then_inc(m_free, 1)
                    dve.wait_ge(m_free, b * 64 * G + 64 * (g + 1))
                    link(v.tensor_reduce(nmx[:, :], mx[:, :, :], AX.X, ALU.max, negate=True))
                    if g >= 1:
                        dve.wait_ge(t_full, b * USES + USE["max", g - 1, 1] + 1)
                    link(v.tensor_copy(mxp[:, :, 0], nmx[:, :]))
                    link(v.tensor_tensor(mxr[:, :], nmx[:, :], mxp[:, :, 0], ALU.subtract))
                    link(v.tensor_copy(mxp[:, :, 1], mxr[:, :]))
                    v.tensor_tensor(mxp[:, :, 2], mxr[:, :], mxp[:, :, 1], ALU.subtract).then_inc(mx_ready, 1)

                def heads_out(g):
                    dve.wait_ge(t_full, b * USES + USE["out", g, 0] + 1)
                    o = bank[6].rearrange("p (t n) -> p t n", n=32)
                    link(v.reciprocal(rec[:, :], o[:, :, HD]))
                    for t in range(QT):
                        ins = v.tensor_tensor(
                            attn[:, t, HG * HD * g:HG * HD * (g + 1)].rearrange("p (j d) -> p j d", d=HD),
                            o[:, HG * t:HG * t + HG, 0:HD],
                            rec[:, HG * t:HG * t + HG, None].broadcast_to((P, HG, HD)), ALU.mult)
                    ins.then_inc(t_free, 1)

                split(0)
                split(1)
                row_maxima(0)
                for g in range(G):
                    if g + 2 < G:
                        split(g + 2)
                    if g >= 1:
                        heads_out(g - 1)
                    if g + 1 < G:
                        row_maxima(g + 1)
                heads_out(G - 1)

                dve.wait_ge(attn_tr, b + 1)
                v.tensor_copy(xnT[:, 0, :], bank[0])
                v.tensor_copy(xnT[:, 1, :], bank[1]).then_inc(attnT_ready, 1)

                def residual(dst, base, k):
                    dve.wait_ge(proj_mm, b * 3 + k + 1)
                    dve.wait_ge(x_based, 1 + b * 3 + k + 1)
                    for i in range(2):
                        ins = v.tensor_tensor(dst[:, 2 * i:2 * i + 2, :].rearrange("p t d -> p (t d)"), bank[2 + i],
                                              base[:, 2 * i:2 * i + 2, :].rearrange("p t d -> p (t d)"), ALU.add)
                    ins.then_inc(x_new, 1)
                    dve.wait_ge(x_new, b * 3 + k + 1)

                residual(xw, xw, 0)
                layer_norm(1, xw)
                xT_copy(1)
                residual(xv, xv, 1)
                layer_norm(2, xv)
                xT_copy(2)
                for t in range(QT):
                    for i in range(4):
                        n = 4 * t + i
                        w_ = min(PW, NK - i * PW)
                        dve.wait_ge(sc_mm, b * 16 + n + 1)
                        v.bn_stats(st1[:, t, i, :], bank[4 + i][:, 0:w_]).then_inc(sc_stat, 1)
                dve.wait_ge(sc_stat, b * 16 + 16)
                v.tensor_copy(rs[:, :], st1[:, :, 0, 0])
                for t in range(QT):
                    ins = v.bn_aggr(mv1[:, t, :], st1[:, t, :, :].rearrange("p a b -> p (a b)"))
                ins.then_inc(sc_var, 1)
                dve.wait_ge(sc_std, b + 1)
                link(v.tensor_scalar(rs[:, :], sg[:, :], 1e-8, None, ALU.add))
                link(v.reciprocal(rs[:, :], rs[:, :]))
                dve.wait_ge(q1_tr, b * 2 + 1)
                v.tensor_tensor(qa[:, :, 0:A1], bank[2][:, 0:QT * A1].rearrange("p (t d) -> p t d", d=A1),
                                rs[:, :, None].broadcast_to((P, QT, A1)), ALU.mult)
                v.scalar_tensor_tensor(out=qa[:, :, 2 * A1], in0=mv1[:, :, 0], scalar=-1.0, in1=rs[:, :],
                                       op0=ALU.mult, op1=ALU.mult).then_inc(qa_ready, 1)
                dve.wait_ge(q1_tr, b * 2 + 2)
                v.tensor_copy(q1a[:, :], bank[3][0:2 * A1 + 1, :]).then_inc(qa_ready, 1)

                dve.wait_ge(proj_mm, b * 3 + 3)
                dve.wait_ge(x_based, 1 + b * 3 + 3)
                for t in range(QT):
                    ins = v.reciprocal(rs[:, t:t + 1], bank[2 + t][:, D:D + 1])
                link(ins)
                for t in range(QT):
                    ins = v.scalar_tensor_tensor(out=xw[:, t, :], in0=bank[2 + t][:, 0:D], scalar=rs[:, t:t + 1],
                                                 in1=xw[:, t, :], op0=ALU.mult, op1=ALU.add)
                ins.then_inc(x_new, 1)
                dve.wait_ge(x_new, b * 3 + 3)
                layer_norm(3, xw)
                xT_copy(3)
                assert count[0] == DVE_STEPS, count


SETUP_DVE = 17 + 1 + 12 + 4 + 4 + 1 + 1
DVE_STEPS_PER_BATCH = 1 + 4 * 2 + 1 + G * 3 + G * 4 + G + 2 + 1


def stage_two(nc, w, x3_d, xn_d, xnT_d, y_d, out, ident, bank_):
    phi_d = w["L1_ffn_phi"].rearrange("(k p) n q -> p k (n q)", p=P)
    NC = NS // SC
    with ExitStack() as st:
        sb = lambda name, shape, dt=F32: st.enter_context(nc.sbuf_tensor(name, shape, dt))
        sem = lambda name: st.enter_context(nc.semaphore(name))
        bank = [t[:, :] for t in bank_]
        negs = sb("negs", [P, B, QT])
        onesr = sb("onesr", [1, P])
        xT = sb("xT", [P, B, 2, S])
        NT = B * NC

        with ExitStack() as s2:
            sb2 = lambda name, shape, dt=F32: s2.enter_context(nc.sbuf_tensor(name, shape, dt))
            sem2 = lambda name: s2.enter_context(nc.semaphore(name))
            disp = sb2("disp", [P, QT, B, SC])
            phi = sb2("phi", [P, 2, SC])
            we = sb2("we", [P, SC // SP_, 2, D])
            be = sb2("be", [P, 2, D])
            bm = sb2("bm", [P, SC])
            bsum = sb2("bsum", [P, SC])
            mxs = sb2("mxs", [P, B])
            xnb = sb2("xnb", [P, 2, QT, D])
            slT = sb2("slT", [P, 2, 2, SC])
            ysb = sb2("ysb", [P, 2, 2, D])
            x_in = sem2("x_in2")
            par_in = sem2("par_in")
            l_mm = sem2("l_mm")
            l_copied = sem2("l_copied")
            first = sem2("first")
            shifted = sem2("shifted")
            exped = sem2("exped")
            summed = sem2("summed")
            normed = sem2("normed")
            dstep = sem2("dstep")
            xn_in = [sem2(f"xn_in{i}") for i in range(2)]
            sl_mm = sem2("sl_mm")
            sl_copied = sem2("sl_copied")
            y_mm = sem2("y_mm")
            y_ready = sem2("y_ready")
            y_stored = [sem2(f"y_stored{i}") for i in range(2)]
            block = s2.enter_context(nc.Block())
            EN = SC // SP_

            @block.sync
            def _(sp):
                for b4 in range(4):
                    sp.dma_start(xT[:, 4 * b4:4 * b4 + 4, :, :],
                                 xnT_d[4 * b4:4 * b4 + 4].rearrange("b p k s -> p b k s")).then_inc(x_in, 16)
                with sp.Fori(0, NC) as s:
                    sp.wait_ge(y_ready, 1 + s * B)
                    sp.dma_start(phi[:, :, :], phi_d[:, :, bass.ds(s * SC, SC)]).then_inc(par_in, 16)
                    sp.dma_start(we[:, :, :, :], w["L1_ffn_W"][bass.ds(s * EN, EN)].rearrange(
                        "n (k p) e -> p n k e", p=P)).then_inc(par_in, 16)
                    for i in range(EN):
                        sp.dma_start(be[32 * (i % 4):32 * (i % 4) + 32, i // 4, :],
                                     w["L1_ffn_b"][bass.ds(s * EN + i, 1), :].broadcast_to((SP_, D)))\
                            .then_inc(par_in, 16)
                    for b in range(B):
                        if b >= 2:
                            sp.wait_ge(sl_mm, 1 + s * B + b - 1)
                        sp.dma_start(xnb[:, b % 2, :, :], xn_d[b].rearrange("(t p) d -> p t d", p=P))\
                            .then_inc(xn_in[b % 2], 16)

            @block.gpsimd
            def _(pool):
                with pool.Fori(0, NC) as s:
                    for t in range(QT):
                        pool.wait_ge(summed, s * QT + t + 1)
                        pool.tensor_tensor(disp[:, t, :, :], disp[:, t, :, :],
                                           bsum[:, None, :].broadcast_to((P, B, SC)), ALU.mult).then_inc(normed, 1)

            @block.tensor
            def _(pe):
                mm = nc.tensor.matmul
                pe.wait_ge(x_in, 64)
                pe.sem_inc(sl_mm, 1)
                with pe.Fori(0, NC) as s:
                    pe.wait_ge(par_in, (s + 1) * 16 * (2 + EN))
                    for t in range(QT):
                        for bb in range(B // 2):
                            n = t * B // 2 + bb
                            if n >= 4:
                                pe.wait_ge(l_copied, s * QT * B // 2 + n - 3)
                            for a in range(2):
                                for k in range(2):
                                    last = mm(bank[n % 4][:, a * SC:(a + 1) * SC],
                                              xT[:, 2 * bb + a, k, t * P:(t + 1) * P], phi[:, k, :],
                                              start=(k == 0), stop=(k == 1))
                            last.then_inc(l_mm, 1)
                    pe.wait_ge(normed, s * QT + QT)

                    def slots(b):
                        pe.wait_ge(xn_in[b % 2], (s * (B // 2) + b // 2 + 1) * 16)
                        if b >= 1:
                            pe.wait_ge(sl_copied, s * B + b)
                        for h in range(2):
                            for t in range(QT):
                                last = mm(bank[4 + h][:, 0:SC], xnb[:, b % 2, t, h * P:(h + 1) * P],
                                          disp[:, t, b, :], start=(t == 0), stop=(t == QT - 1))
                        last.then_inc(sl_mm, 1)

                    def experts(b):
                        pe.wait_ge(sl_copied, s * B + b + 1)
                        if b >= 1:
                            pe.wait_ge(y_ready, 1 + s * B + b)
                        for a in range(SC // P):
                            for k in range(2):
                                for j in range(4):
                                    c0 = a * P + 32 * j
                                    last = mm(bank[6 + a][32 * j:32 * j + 32, 0:D], slT[:, b % 2, k, c0:c0 + 32],
                                              we[:, 4 * a + j, k, :], start=(k == 0), stop=(k == 1),
                                              skip_group_check=True)
                        last.then_inc(y_mm, 1)

                    slots(0)
                    for b in range(B):
                        if b + 1 < B:
                            slots(b + 1)
                        experts(b)

            @block.scalar
            def _(act):
                fn = nc.scalar.activation
                for i in range(2):
                    act.sem_inc(y_stored[i], 1)
                with act.Fori(0, NC) as s:
                    def store_y(b):
                        act.wait_ge(y_ready, 1 + s * B + b + 1)
                        act.dma_start(y_d[b, bass.ds(s * SC, SC), :].rearrange("(a p) e -> p a e", p=P),
                                      ysb[:, b % 2, :, :]).then_inc(y_stored[b % 2], 16)

                    act.wait_ge(sl_mm, 1 + s * B)
                    for t in range(QT):
                        for bb in range(B // 2):
                            n = t * B // 2 + bb
                            act.wait_ge(l_mm, s * QT * B // 2 + n + 1)
                            fn(disp[:, t, 2 * bb:2 * bb + 2, :].rearrange("p a n -> p (a n)"), bank[n % 4],
                               ACT.Copy).then_inc(l_copied, 1)
                        if t >= 1:
                            act.wait_ge(shifted, s * QT + t)
                            fn(disp[:, t - 1, :, :], disp[:, t - 1, :, :], ACT.Exp).then_inc(exped, 1)
                    act.wait_ge(shifted, s * QT + QT)
                    fn(disp[:, QT - 1, :, :], disp[:, QT - 1, :, :], ACT.Exp).then_inc(exped, 1)
                    for b in range(B):
                        act.wait_ge(sl_mm, 1 + s * B + b + 1)
                        if b >= 2:
                            act.wait_ge(y_mm, s * B + b - 1)
                        for h in range(2):
                            e = fn(slT[:, b % 2, h, :], bank[4 + h][:, 0:SC], ACT.Copy)
                        e.then_inc(sl_copied, 1)
                        if b >= 1:
                            store_y(b - 1)
                    store_y(B - 1)
                for i in range(2):
                    act.wait_ge(y_stored[i], 1 + 16 * NT // 2)

            @block.vector
            def _(dve):
                v = nc.vector
                v.memset(onesr[:, :], 1.0)
                v.memset(negs[:, :, :], -3.0e38).then_inc(first, 1)
                dve.wait_ge(first, 1)
                dve.sem_inc(y_ready, 1)
                PER = QT * 3
                with dve.Fori(0, NC) as s:
                    count = [0]

                    def link(ins):
                        count[0] += 1
                        ins.then_inc(dstep, 1)
                        dve.wait_ge(dstep, s * PER + count[0])

                    def shift(t):
                        dve.wait_ge(l_copied, s * QT * B // 2 + (t + 1) * B // 2)
                        v.tensor_reduce(mxs[:, :], disp[:, t, :, :], AX.X, ALU.max)
                        link(v.tensor_reduce(bm[:, :], disp[:, t, :, :].rearrange("p b n -> p n b"), AX.X, ALU.max))
                        v.tensor_tensor(disp[:, t, :, :], disp[:, t, :, :],
                                        bm[:, None, :].broadcast_to((P, B, SC)), ALU.subtract).then_inc(shifted, 1)
                        link(v.tensor_tensor(negs[:, :, t], negs[:, :, t], mxs[:, :], ALU.max))

                    def total(t):
                        dve.wait_ge(exped, s * QT + t + 1)
                        if t >= 1:
                            dve.wait_ge(normed, s * QT + t)
                        link(v.tensor_reduce(bsum[:, :], disp[:, t, :, :].rearrange("p b n -> p n b"), AX.X, ALU.add))
                        v.reciprocal(bsum[:, :], bsum[:, :]).then_inc(summed, 1)

                    shift(0)
                    for t in range(QT):
                        if t + 1 < QT:
                            shift(t + 1)
                        total(t)
                    for b in range(B):
                        dve.wait_ge(y_mm, s * B + b + 1)
                        dve.wait_ge(y_stored[b % 2], 1 + (s * (B // 2) + b // 2) * 16)
                        for a in range(2):
                            ins = v.tensor_tensor(ysb[:, b % 2, a, :], bank[6 + a][:, 0:D], be[:, a, :], ALU.add)
                        ins.then_inc(y_ready, 1)
                    assert count[0] == PER

        with ExitStack() as s3:
            sb3 = lambda name, shape, dt=F32: s3.enter_context(nc.sbuf_tensor(name, shape, dt))
            sem3 = lambda name: s3.enter_context(nc.semaphore(name))
            KS = NS // P
            phi = sb3("phi_all", [P, 2, NS])
            ya = sb3("ya", [P, KS, D + 1])
            x3 = sb3("x3", [P, QT, D])
            xc = sb3("xc", [P, 2, S])
            ng = sb3("ng", [P, QT])
            ngr = sb3("ngr", [1, S])
            ex = sb3("ex", [P, 3, S])
            rc = sb3("rc", [P, QT])
            par = sem3("par3")
            y_in = sem3("y_in")
            x_in = sem3("x_in3")
            made = sem3("made3")
            n_ready = sem3("n_ready")
            n_tr = sem3("n_tr")
            nr_ready = sem3("nr_ready")
            c_mm = sem3("c_mm")
            c_exp = sem3("c_exp")
            o_mm = sem3("o_mm")
            o_rc = sem3("o_rc")
            o_ready = sem3("o_ready")
            o_stored = sem3("o_stored")
            block = s3.enter_context(nc.Block())

            @block.sync
            def _(sp):
                sp.dma_start(phi[:, :, :], phi_d).then_inc(par, 16)
                sp.sem_inc(o_stored, 1)
                with sp.Fori(0, B) as b:
                    sp.wait_ge(o_mm, 1 + b * KS)
                    sp.dma_start(ya[:, :, 0:D], y_d[b].rearrange("(c p) e -> p c e", p=P)).then_inc(y_in, 16)
                    sp.wait_ge(o_stored, 1 + b * 16)
                    sp.dma_start(x3[:, :, :], x3_d[b].rearrange("(t p) d -> p t d", p=P)).then_inc(x_in, 16)
                    sp.wait_ge(o_ready, 1 + b + 1)
                    sp.dma_start(out[b].rearrange("(t p) d -> p t d", p=P), x3[:, :, :]).then_inc(o_stored, 16)
                sp.wait_ge(o_stored, 1 + 16 * B)

            @block.tensor
            def _(pe):
                mm = nc.tensor.matmul
                pe.wait_ge(par, 16)
                pe.wait_ge(made, 1)
                pe.sem_inc(o_mm, 1)
                with pe.Fori(0, B) as b:
                    pe.wait_ge(n_ready, b + 1)
                    for t in range(QT):
                        last = nc.tensor.transpose(bank[0][0:1, t * P:(t + 1) * P], ng[:, t:t + 1], ident[:, :])
                    last.then_inc(n_tr, 1)
                    pe.wait_ge(nr_ready, b + 1)
                    for c in range(KS + 2):
                        if c < KS:
                            if c >= 4:
                                pe.wait_ge(c_exp, b * KS + c - 3)
                            o = bank[c % 4]
                            for k in range(2):
                                mm(o, phi[:, k, c * P:(c + 1) * P], xc[:, k, :], start=(k == 0), stop=False)
                            mm(o, onesr[:, :], ngr[:, :], start=False, stop=True).then_inc(c_mm, 1)
                        if c >= 2:
                            e = c - 2
                            if e == 0:
                                pe.wait_ge(y_in, b * 16 + 16)
                                pe.wait_ge(o_ready, 1 + b)
                            pe.wait_ge(c_exp, b * KS + e + 1)
                            for t in range(QT):
                                last = mm(bank[4 + t][:, 0:D + 1], ex[:, e % 3, t * P:(t + 1) * P], ya[:, e, :],
                                          start=(e == 0), stop=(e == KS - 1))
                            last.then_inc(o_mm, 1)

            @block.scalar
            def _(act):
                with act.Fori(0, B) as b:
                    for c in range(KS):
                        act.wait_ge(c_mm, b * KS + c + 1)
                        if c >= 3:
                            act.wait_ge(o_mm, 1 + b * KS + c - 2)
                        nc.scalar.activation(ex[:, c % 3, :], bank[c % 4], ACT.Exp).then_inc(c_exp, 1)

            @block.vector
            def _(dve):
                v = nc.vector
                v.memset(ya[:, :, D:D + 1], 1.0).then_inc(made, 1)
                dve.sem_inc(o_ready, 1)
                with dve.Fori(0, B) as b:
                    v.tensor_scalar(ng[:, :, None], negs[:, bass.ds(b, 1), :].rearrange("p a t -> p t a"), -1.0, None,
                                    ALU.mult).then_inc(n_ready, 1)
                    v.tensor_copy(xc[:, :, :], xT[:, bass.ds(b, 1), :, :].rearrange("p a k s -> p (a k) s"))
                    dve.wait_ge(n_tr, b + 1)
                    v.tensor_copy(ngr[:, :], bank[0][0:1, :]).then_inc(nr_ready, 1)
                    dve.wait_ge(o_mm, 1 + b * KS + KS)
                    dve.wait_ge(x_in, b * 16 + 16)
                    for t in range(QT):
                        ins = v.reciprocal(rc[:, t:t + 1], bank[4 + t][:, D:D + 1])
                    ins.then_inc(o_rc, 1)
                    dve.wait_ge(o_rc, b + 1)
                    for t in range(QT):
                        ins = v.scalar_tensor_tensor(out=x3[:, t, :], in0=bank[4 + t][:, 0:D], scalar=rc[:, t:t + 1],
                                                     in1=x3[:, t, :], op0=ALU.mult, op1=ALU.add)
                    ins.then_inc(o_ready, 1)


_INS = ['x', 'ctx_1024', 'mask_BxS2_bk0', 'L0_xattn_Wq', 'L0_xattn_Wkv', 'L0_xattn_Wp', 'L0_xattn_bp',
        'L0_xattn_ln_g', 'L0_xattn_ln_b', 'L0_ffn_U1', 'L0_ffn_V1', 'L0_ffn_b1', 'L0_ffn_U2', 'L0_ffn_V2',
        'L0_ffn_b2', 'L1_xattn_Wq', 'L1_xattn_bq', 'L1_xattn_Wk', 'L1_xattn_bk', 'L1_xattn_Wv', 'L1_xattn_bv',
        'L1_xattn_Wout', 'L1_xattn_bout', 'L1_ffn_phi', 'L1_ffn_W', 'L1_ffn_b']


def kernel(**inputs):
    import numpy as _np
    import concourse.bacc as _bacc
    from concourse import mybir as _mybir
    from concourse.bass_utils import run_bass_kernel_spmd as _run

    nc = _bacc.Bacc("TRN2", target_bir_lowering=False, num_devices=1)
    arrays, args = {}, {}
    for name in _INS:
        a = _np.ascontiguousarray(inputs[name])
        if a.dtype.kind == "b":
            a = a.astype(_np.int32)
        arrays[f"in_{name}"] = a
        args[name] = nc.dram_tensor(f"in_{name}", a.shape, _mybir.dt.from_np(a.dtype), kind="ExternalInput").ap()
    out = nc.dram_tensor("out_0", (B, S, D), F32, kind="ExternalOutput").ap()
    x3_d = nc.dram_tensor("x3_scratch", (B, S, D), F32, kind="Internal").ap()
    xn_d = nc.dram_tensor("xn_scratch", (B, S, D), F32, kind="Internal").ap()
    xnT_d = nc.dram_tensor("xnT_scratch", (B, P, 2, S), F32, kind="Internal").ap()
    y_d = nc.dram_tensor("y_scratch", (B, NS, D), F32, kind="Internal").ap()
    layers(nc, args["x"], args["ctx_1024"], args["mask_BxS2_bk0"], args, x3_d, xn_d, xnT_d, y_d, out)
    r = _run(nc, [arrays], core_ids=[0])
    return r.results[0]["out_0"]
```

```python
from contextlib import ExitStack

import concourse.bass as bass
from concourse import mybir

ALU = mybir.AluOpType
ACT = mybir.ActivationFunctionType
AX = mybir.AxisListType
F32 = mybir.dt.float32
BF16 = mybir.dt.bfloat16
I32 = mybir.dt.int32

P = 128
B, S, D = 16, 512, 256
NK = 1601
QT = S // P
KC = -(-NK // P)
KL = NK - (KC - 1) * P
H, HD = 16, 16
HG = 4
G = H // HG
TT = KC + QT
NP = 6 * HD
NR = NP + 3
PW = -(-NK // 4)
RANK, FF = 64, 1024
FC = FF // P
A1 = 16
NS, SP_, NE = 2048, 32, 64
R1 = 65
SC = 256
EPS = 1e-5


def key_rows(c):
    return P if c < KC - 1 else KL


def transpose_bank_uses():
    order = []
    stack = lambda g: [("stack", g, u) for u in range(10)]
    order += stack(0) + stack(1) + [("max", 0, u) for u in range(2)]
    for g in range(G):
        if g > 0:
            order.append(("out", g - 1, 0))
        if g + 2 < G:
            order += stack(g + 2)
        if g + 1 < G:
            order += [("max", g + 1, u) for u in range(2)]
    order.append(("out", G - 1, 0))
    return {use: n for n, use in enumerate(order)}


USE = transpose_bank_uses()
USES = len(USE)


def layers(nc, x, ctx_in, mask, w, x3_d, xn_d, xnT_d, y_d, out):
    with ExitStack() as keep:
        sbk = lambda name, shape, dt=F32: keep.enter_context(nc.sbuf_tensor(name, shape, dt))
        ident = sbk("ident", [P, P])
        psum = keep.enter_context(nc.psum_tensor("psum", [P, 8, 512], F32))
        stage_one(nc, x, ctx_in, mask, w, x3_d, xn_d, xnT_d, ident, psum)
        stage_two(nc, w, x3_d, xn_d, xnT_d, y_d, out, ident, psum)


WOVEN = (
    ["ctxT0", "attnT", ("ctx", 0), "proj"] + [("ctx", 1), ("ctx", 2), ("ctx", 3), "x1T", ("ctx", 4), "u1", ("ctx", 5)]
    + [z for f in range(FC + 2) for z in ([("ffn", f), ("ctx", 6 + f // 2)] if f % 2 == 0 and f < 8 else [("ffn", f)])]
    + ["v2", ("ctx", 10), ("ctx", 11), ("ctx", 12), "norm", "x2T", "q1"]
    + [("sc", t) for t in range(QT)] + ["qtr", "stack0", "qaT"]
    + [z for c in range(KC + 2) for z in (("s1", c), ("rows", c))]
    + ["kv1", ("rows", 15), "out", "max0", "x3T"])
HEAD = {"ctxT0", "norm", "stack0", "max0", "kv1"} | {("ctx", c) for c in range(KC)} | {("rows", r) for r in range(16)}


def run_woven(tail, head):
    for label in WOVEN:
        steps = head if label in HEAD else tail
        if steps is not None and label in steps:
            steps[label]()


def stage_one(nc, x, ctx_d, mask, w, x3_d, xn_d, xnT_d, ident, psum):
    with ExitStack() as st:
        sb = lambda name, shape, dt=F32: st.enter_context(nc.sbuf_tensor(name, shape, dt))
        sem = lambda name: st.enter_context(nc.semaphore(name))
        bank = [psum[:, i, :] for i in range(8)]

        identb = sb("identb", [P, P], BF16)
        wq = sb("wq", [P, 2, D])
        wkv = sb("wkv", [P, 2, 2 * D])
        wp = sb("wp", [P, 2, D])
        u1 = sb("u1", [P, 2, RANK])
        v1 = sb("v1", [RANK, FF])
        u2 = sb("u2", [P, FC, RANK])
        v2 = sb("v2", [RANK, D])
        b1c = sb("b1c", [P, FC])
        w1q = sb("w1q", [P, 2, A1])
        w1kv = sb("w1kv", [P, 2, 2 * A1])
        bq = sb("bq", [A1, 1])
        bkv = sb("bkv", [2 * A1, 1])
        wst = sb("wst", [P, D + 1])
        bpr = sb("bpr", [P, D])
        b2r = sb("b2r", [P, D])
        bor = sb("bor", [P, D])
        lng = sb("lng", [P, HD])
        lnb = sb("lnb", [P, HD])
        eps = sb("eps", [P, 1])
        mean_w = sb("mean_w", [P, 4, H])
        maskb = sb("maskb", [P, KC, B])

        ctx_sb = sb("ctx_sb", [P, KC, D])
        ctxT = sb("ctxT", [P, 2, KC * P])
        vaug = sb("vaug", [P, KC, H, HD + 1])
        kraw = sb("kraw", [P, TT, D])
        sq = sb("sq", [P, 4, D])
        ssq = sb("ssq", [P, TT, H])
        rstd = sb("rstd", [P, TT, H])
        kf = sb("kf", [P, TT, HG * HD])
        stack = [ctx_sb[:, :, :].rearrange("p a k -> p (a k)").bitcast(BF16)[:, 0:TT * HG * NP].rearrange(
            "p (t n) -> p t n", n=NP), sb("stack1", [P, TT * HG, NP], BF16)[:, :, :]]
        kst = [sb(f"kst{i}", [P, HG, KC * P], BF16) for i in range(3)]
        qst = [sb(f"qst{i}", [P, HG, S], BF16) for i in range(3)]
        mx = sb("mx", [P, HG * QT, 4])
        nmx = sb("nmx", [P, HG * QT])
        mxr = sb("mxr", [P, HG * QT])
        mxp = sb("mxp", [P, HG * QT, 4], BF16)
        probs = sb("probs", [P, 4, 1024])
        hT = probs[:, :, :].rearrange("p a b -> p (a b)").rearrange("p (f q) -> p f q", f=FC)
        o_sb = sb("o_sb", [P, S])
        rec = sb("rec", [P, QT * HG])
        attn = sb("attn", [P, QT, D])
        xin = sb("xin", [P, QT, D])
        xw = sb("xw", [P, QT, D])
        xv = sb("xv", [P, QT, D])
        xn = sb("xn", [P, QT, D])
        xnT = sb("xnT", [P, 2, S])
        xn0 = kf[:, :, :].rearrange("p t d -> p (t d)")[:, 0:QT * D].rearrange("p (t d) -> p t d", d=D)
        xn0T = sq[:, :, :].rearrange("p (k a) d -> p k (a d)", k=2)
        bst0 = sb("bst0", [P, QT, 6])
        mv0 = sb("mv0", [P, QT, 2])
        std0 = sb("std0", [P, QT])
        rs0 = sb("rs0", [P, QT])
        bst = sb("bst", [P, QT, 6])
        mv = sb("mv", [P, QT, 2])
        std = sb("std", [P, QT])
        rs = sb("rs", [P, QT])
        pT = o_sb[0:RANK, :]
        kv1T = sb("kv1T", [R1, NK])
        v1a = sb("v1a", [P, KC, 2 * A1])
        qa = sb("qa", [P, QT, R1])
        q1T = sb("q1T", [R1, S])
        q1a = attn[0:R1, 2:4, :].rearrange("p a d -> p (a d)")
        st1 = sb("st1", [P, QT, 4, 6])
        mv1 = sb("mv1", [P, QT, 2])
        sg = sb("sg", [P, QT])
        maskcol = sb("maskcol", [P, KC])

        weights_in = sem("weights_in")
        ident_made = sem("ident_made")
        setup_dve = sem("setup_dve")
        setup_pool = sem("setup_pool")
        setup_pe = sem("setup_pe")
        ctx_loaded = sem("ctx_loaded")
        x_loaded = sem("x_loaded")
        x_based = sem("x_based")
        ln0_var = sem("ln0_var")
        ln0_std = sem("ln0_std")
        xn0_ready = sem("xn0_ready")
        xn0T_mm = sem("xn0T_mm")
        xn0T_ready = sem("xn0T_ready")
        ln_var = sem("ln_var")
        ln_std = sem("ln_std")
        xn_ready = sem("xn_ready")
        xnT_mm = sem("xnT_mm")
        xnT_ready = sem("xnT_ready")
        q_mm = sem("q_mm")
        q_raw = sem("q_raw")
        ctx_tr = sem("ctx_tr")
        ctxT_ready = sem("ctxT_ready")
        kv_mm = sem("kv_mm")
        kv_raw = sem("kv_raw")
        sq_summed = sem("sq_summed")
        head_std = sem("head_std")
        head_rstd = sem("head_rstd")
        kv1_mm = sem("kv1_mm")
        kv1_ready = sem("kv1_ready")
        v1_tr = sem("v1_tr")
        v1_ready = sem("v1_ready")
        pool_step = sem("pool_step")
        kf_ready = sem("kf_ready")
        stack_ready = sem("stack_ready")
        t_full = sem("t_full")
        t_free = sem("t_free")
        m_full = sem("m_full")
        m_free = sem("m_free")
        mx_ready = sem("mx_ready")
        s_full = sem("s_full")
        s_exp = sem("s_exp")
        pv_mm = sem("pv_mm")
        o_copied = sem("o_copied")
        attn_tr = sem("attn_tr")
        attnT_ready = sem("attnT_ready")
        proj_mm = sem("proj_mm")
        x_new = sem("x_new")
        ffn_mm = sem("ffn_mm")
        ffn_act = sem("ffn_act")
        h_mm = sem("h_mm")
        h_act = sem("h_act")
        q1_mm = sem("q1_mm")
        q1_act = sem("q1_act")
        sc_mm = sem("sc_mm")
        sc_stat = sem("sc_stat")
        sc_var = sem("sc_var")
        sc_std = sem("sc_std")
        q1_tr = sem("q1_tr")
        qa_ready = sem("qa_ready")
        s1_mm = sem("s1_mm")
        s1_exp = sem("s1_exp")
        pv1_mm = sem("pv1_mm")
        o_copied_1 = sem("o_copied_1")
        first_step = sem("first_step")
        head_step = sem("head_step")
        attention_step = sem("attention_step")
        tail_step = sem("tail_step")
        stored = sem("stored")

        POOL_STEPS = 2 * G
        NW = 32

        block = st.enter_context(nc.Block())

        @block.sync
        def _(sp):
            loads = [
                (wq[:, :, :], w["L0_xattn_Wq"].rearrange("(k p) n -> p k n", p=P)),
                (wkv[:, :, :], w["L0_xattn_Wkv"].rearrange("(k p) n -> p k n", p=P)),
                (wp[:, :, :], w["L0_xattn_Wp"].rearrange("(k p) n -> p k n", p=P)),
                (u1[:, :, :], w["L0_ffn_U1"].rearrange("(k p) n -> p k n", p=P)),
                (v1[:, :], w["L0_ffn_V1"]),
                (u2[:, :, :], w["L0_ffn_U2"].rearrange("(k p) n -> p k n", p=P)),
                (v2[:, :], w["L0_ffn_V2"]),
                (b1c[:, :], w["L0_ffn_b1"].rearrange("(k p) -> p k", p=P)),
                (w1q[:, :, :], w["L1_xattn_Wq"].rearrange("(k p) n -> p k n", p=P)),
                (w1kv[:, :, 0:A1], w["L1_xattn_Wk"].rearrange("(k p) n -> p k n", p=P)),
                (w1kv[:, :, A1:2 * A1], w["L1_xattn_Wv"].rearrange("(k p) n -> p k n", p=P)),
                (bq[:, :], w["L1_xattn_bq"].rearrange("(p a) -> p a", a=1)),
                (bkv[0:A1, :], w["L1_xattn_bk"].rearrange("(p a) -> p a", a=1)),
                (bkv[A1:2 * A1, :], w["L1_xattn_bv"].rearrange("(p a) -> p a", a=1)),
                (bpr[:, :], w["L0_xattn_bp"].partition_broadcast(P)),
                (b2r[:, :], w["L0_ffn_b2"].partition_broadcast(P)),
                (bor[:, :], w["L1_xattn_bout"].partition_broadcast(P)),
                (lng[:, :], w["L0_xattn_ln_g"].partition_broadcast(P)),
                (lnb[:, :], w["L0_xattn_ln_b"].partition_broadcast(P)),
            ]
            for j in range(4):
                loads.append((probs[32 * j:32 * j + A1, :, :].rearrange("p a b -> p (a b)").rearrange(
                    "p (h n) -> p h n", h=H), w["L1_xattn_Wout"].rearrange("(h p) n -> p h n", p=A1)))
            loads.append((kraw[0:B, 0:7, :].rearrange("p a b -> p (a b)").bitcast(I32)[:, 0:NK], mask))
            for dst, src in loads:
                sp.dma_start(dst, src, allow_slow_non_contiguous=True).then_inc(weights_in, 16)
            assert len(loads) <= NW
            sp.wait_ge(weights_in, 16 * len(loads))
            sp.wait_ge(setup_dve, SETUP_DVE)
            sp.wait_ge(setup_pool, 4)

            def load_context(b):
                sp.dma_start(ctx_sb[:, 0:KC - 1, :],
                             ctx_d[b, 0:(KC - 1) * P, :].rearrange("(c p) d -> p c d", p=P)).then_inc(ctx_loaded, 16)
                sp.dma_start(ctx_sb[0:KL, KC - 1, :], ctx_d[b, (KC - 1) * P:NK, :]).then_inc(ctx_loaded, 16)

            def load_x(b):
                sp.dma_start(xin[:, :, :], x[b].rearrange("(t p) d -> p t d", p=P)).then_inc(x_loaded, 16)

            load_context(0)
            load_x(0)
            with sp.Fori(1, B) as b:
                sp.wait_ge(x_based, 1 + (b - 1) * 3 + 1)
                load_x(b)
                sp.wait_ge(t_full, (b - 1) * USES + USE["stack", 2, 9] + 1)
                load_context(b)
            sp.wait_ge(x_based, 1 + (B - 1) * 3 + 1)
            load_x(B - 1)
            sp.wait_ge(x_loaded, (B + 1) * 16)
            sp.wait_ge(stored, 1 + 48 * B)

        NLOAD = 19 + 4 + 1

        @block.gpsimd
        def _(pool):
            pool.memset(ident[:, :], 0.0).then_inc(ident_made, 1)
            pool.wait_ge(ident_made, 1)
            pool.affine_select(out=ident[:, :], in_=ident[:, :], compare_op=ALU.not_equal, fill=1.0,
                               base=0, pattern=[[-1, P]], channel_multiplier=1).then_inc(ident_made, 1)
            pool.wait_ge(ident_made, 2)
            pool.tensor_copy(identb[:, :], ident[:, :]).then_inc(ident_made, 1)
            pool.wait_ge(ident_made, 3)
            for i in range(3):
                pool.memset(kst[i][96:NR, :, :], 1.0).then_inc(setup_pool, 1)
                pool.wait_ge(setup_pool, i + 1)
            pool.memset(eps[:, :], EPS).then_inc(setup_pool, 1)
            pool.wait_ge(setup_pool, 4)
            pool.sem_inc(x_based, 1)

            def normalised(b, g):
                pool.wait_ge(head_rstd, b + 1)
                if g >= 1:
                    pool.wait_ge(stack_ready, b * G + g)
                hs = slice(HG * g, HG * g + HG)
                kin = kraw[:, :, HG * HD * g:HG * HD * (g + 1)].rearrange("p t (h d) -> p t h d", h=HG)
                kfv = kf[:, :, :].rearrange("p t (h d) -> p t h d", h=HG)
                pool.tensor_tensor(kfv, kin, rstd[:, :, hs, None].broadcast_to((P, TT, HG, HD)),
                                   ALU.mult).then_inc(pool_step, 1)
                pool.wait_ge(pool_step, b * POOL_STEPS + 2 * g + 1)
                kf3 = kf[:, :, :].rearrange("p t (h d) -> p (t h) d", h=HG)
                pool.tensor_tensor(kf3, kf3, lng[:, None, :].broadcast_to((P, TT * HG, HD)),
                                   ALU.mult).then_inc(pool_step, 1)
                pool.wait_ge(pool_step, b * POOL_STEPS + 2 * g + 2)
                pool.tensor_tensor(kf3, kf3, lnb[:, None, :].broadcast_to((P, TT * HG, HD)),
                                   ALU.add).then_inc(kf_ready, 1)

            def head(b):
                return {"norm": lambda: normalised(b, 0), ("rows", 0): lambda: normalised(b, 1)}

            def attention(b):
                normalised(b, 2)
                pool.wait_ge(x_loaded, b * 16 + 16)
                pool.wait_ge(stored, 1 + b * 48)
                pool.tensor_tensor(xw[:, :, :], xin[:, :, :],
                                   bpr[:, None, :].broadcast_to((P, QT, D)), ALU.add).then_inc(x_based, 1)
                normalised(b, 3)

            def tail(b):
                def base(k, dst, src, bias):
                    pool.wait_ge(x_new, b * 3 + k)
                    pool.tensor_tensor(dst[:, :, :], src[:, :, :],
                                       bias[:, None, :].broadcast_to((P, QT, D)), ALU.add).then_inc(x_based, 1)
                return {"x1T": lambda: base(1, xv, xw, b2r), "x2T": lambda: base(2, xw, xv, bor)}

            run_woven(None, head(0))
            attention(0)
            with pool.Fori(1, B) as b:
                run_woven(tail(b - 1), head(b))
                attention(b)
            run_woven(tail(B - 1), None)
            pool.wait_ge(stored, 1 + 48 * B)

        @block.tensor
        def _(pe):
            mm = nc.tensor.matmul
            tr = nc.tensor.transpose
            pe.wait_ge(ident_made, 3)
            pe.wait_ge(setup_dve, SETUP_DVE)
            pe.wait_ge(setup_pool, 4)
            for c in range(KC):
                m = key_rows(c)
                last = tr(bank[0][0:m, B * c:B * c + B], ctxT[0:B, 0, c * P:c * P + m], ident[0:B, 0:B])
            last.then_inc(setup_pe, 1)
            pe.wait_ge(setup_dve, SETUP_DVE + 1)

            def first_norm(b):
                pe.wait_ge(xn0_ready, b + 1)
                for h in range(2):
                    for t in range(QT):
                        last = tr(bank[4 + h][:, t * P:(t + 1) * P], xn0[:, t, h * P:(h + 1) * P], ident[:, :])
                last.then_inc(xn0T_mm, 1)

            def queries(b):
                pe.wait_ge(xn0T_ready, b + 1)
                for t in range(QT):
                    for k in range(2):
                        last = mm(bank[4 + t // 2][:, (t % 2) * D:(t % 2 + 1) * D],
                                  xn0T[:, k, t * P:(t + 1) * P], wq[:, k, :], start=(k == 0), stop=(k == 1))
                last.then_inc(q_mm, 1)

            def head(b):
                def transpose_ctx(c):
                    m = key_rows(c)
                    if c == 0:
                        pe.wait_ge(ctx_loaded, b * 32 + 32)
                        pe.wait_ge(q_raw, b + 1)
                    if c >= 2:
                        pe.wait_ge(ctxT_ready, b * KC + c - 1)
                    for h in range(2):
                        last = tr(bank[4 + c % 2][:, h * P:h * P + m], ctx_sb[0:m, c, h * P:(h + 1) * P],
                                  ident[0:m, 0:m])
                    last.then_inc(ctx_tr, 1)

                def context(c):
                    if c + 1 < KC:
                        transpose_ctx(c + 1)
                    m = key_rows(c)
                    pe.wait_ge(ctxT_ready, b * KC + c + 1)
                    if c >= 2:
                        pe.wait_ge(kv_raw, b * KC + c - 1)
                    for k in range(2):
                        last = mm(bank[6 + c % 2][0:m, :], ctxT[:, k, c * P:c * P + m], wkv[:, k, :],
                                  start=(k == 0), stop=(k == 1))
                    last.then_inc(kv_mm, 1)

                def first_stack():
                    pe.wait_ge(kv_raw, b * KC + KC)
                    for u in range(10):
                        stack_unit(b, 0, u)

                def rows(r):
                    for u in range(4 * r, 4 * r + 4):
                        score_rows(b, 0, u)
                        if u % 4 == 3 and u >= 27:
                            stack_unit(b, 1, (u - 27) // 4)

                def first_max():
                    for u in range(2):
                        max_unit(b, 0, u)

                def layer_one_keys():
                    for i in range(4):
                        n = min(PW, NK - i * PW)
                        if i >= 2:
                            pe.wait_ge(kv1_ready, b * 4 + i - 1)
                        for k in range(2):
                            last = mm(bank[i % 2][0:2 * A1, 0:n], w1kv[:, k, :], ctxT[:, k, i * PW:i * PW + n],
                                      start=(k == 0), stop=(k == 1))
                        last.then_inc(kv1_mm, 1)
                    pe.wait_ge(kv1_ready, b * 4 + 4)
                    tr(bank[1][:, 0:P], ident[:, :], ident[:, :])
                    for c in range(KC):
                        m = key_rows(c)
                        last = tr(bank[0][0:m, 32 * c:32 * c + 32], kv1T[0:32, c * P:c * P + m], ident[0:32, 0:32])
                    last.then_inc(v1_tr, 1)

                steps = {"ctxT0": lambda: transpose_ctx(0), "stack0": first_stack, "max0": first_max,
                         "kv1": layer_one_keys}
                steps.update({("ctx", c): (lambda c=c: context(c)) for c in range(KC)})
                steps.update({("rows", r): (lambda r=r: rows(r)) for r in range(16)})
                return steps

            tb = bank[6].bitcast(BF16)

            def stack_unit(b, g, u, between=None):
                n = USE["stack", g, u]
                if u == 0:
                    pe.wait_ge(stack_ready, b * G + g + 1)
                pe.wait_ge(t_free, 1 + b * USES + n)
                j, half = u // 2, u % 2
                if u < 8:
                    tiles = [(t, j) for t in (range(8) if half == 0 else range(8, KC))]
                else:
                    tiles = [(KC + t, 2 * (u - 8) + a) for a in range(2) for t in range(QT)]
                for i, (t, hj) in enumerate(tiles):
                    m = KL if t == KC - 1 else P
                    last = tr(tb[0:NP, i * P:i * P + m], stack[g % 2][0:m, t * HG + hj, :], identb[0:m, 0:m])
                    if i == 3 and between is not None:
                        between()
                last.then_inc(t_full, 1)

            def max_unit(b, g, u):
                n = USE["max", g, u]
                if u == 0:
                    pe.wait_ge(mx_ready, b * G + g + 1)
                pe.wait_ge(t_free, 1 + b * USES + n)
                for i in range(2 * QT):
                    last = tr(tb[96:NR, i * P:(i + 1) * P], mxp[:, 2 * QT * u + i, 0:3], identb[:, :])
                last.then_inc(t_full, 1)

            def out_unit(b, g):
                n = USE["out", g, 0]
                pe.wait_ge(o_copied, b * G + g + 1)
                pe.wait_ge(t_free, 1 + b * USES + n)
                for t in range(QT):
                    last = tr(bank[6][:, t * P:(t + 1) * P], o_sb[:, t * P:(t + 1) * P], ident[:, :])
                last.then_inc(t_full, 1)

            def score_rows(b, g, u):
                n = 64 * g + u
                j, t, i = u // 16, (u // 4) % 4, u % 4
                if u == 0:
                    pe.wait_ge(t_free, 1 + b * USES + USE["stack", g, 9] + 1)
                if n >= 2:
                    pe.wait_ge(m_free, b * 64 * G + n - 1)
                k0 = min(i * PW, NK - PW)
                mm(bank[4 + n % 2][:, 0:PW], qst[g % 3][0:NP, j, t * P:(t + 1) * P],
                   kst[g % 3][0:NP, j, k0:k0 + PW], start=True, stop=True).then_inc(m_full, 1)

            def score_cols(b, g, c, i):
                m = key_rows(c)
                n = 2 * (KC * g + c) + i
                if n >= 2:
                    pe.wait_ge(s_exp, b * 2 * KC * G + n - 1)
                for a in range(2):
                    j = 2 * i + a
                    last = mm(bank[2 * i + a][0:m, :], kst[g % 3][0:NR, j, c * P:c * P + m],
                              qst[g % 3][0:NR, j, :], start=True, stop=True)
                last.then_inc(s_full, 1)

            def weigh_values(b, g, c):
                m = key_rows(c)
                pe.wait_ge(s_exp, b * 2 * KC * G + 2 * (KC * g + c) + 2)
                if c == 0 and g >= 1:
                    pe.wait_ge(o_copied, b * G + g)
                for j in range(HG):
                    last = mm(bank[7][32 * j:32 * j + HD + 1, :], vaug[0:m, c, HG * g + j, :],
                              probs[0:m, (2 * c + j // 2) % 4, (j % 2) * 512:(j % 2 + 1) * 512],
                              start=(c == 0), stop=(c == KC - 1), skip_group_check=True)
                last.then_inc(pv_mm, 1)

            def attention(b):
                pe.wait_ge(xnT_ready, 1 + b * 3)
                pe.wait_ge(v1_ready, b + 1)
                for g in range(G):
                    pe.wait_ge(t_free, 1 + b * USES + USE["max", g, 1] + 1)
                    done = [0]

                    def piece():
                        if g + 1 < G and done[0] < 64:
                            score_rows(b, g + 1, done[0])
                            done[0] += 1

                    for c in range(KC):
                        score_cols(b, g, c, 0)
                        if c == 0 and g >= 1:
                            out_unit(b, g - 1)
                        piece()
                        score_cols(b, g, c, 1)
                        piece()
                        if 2 <= c < 12 and g + 2 < G:
                            stack_unit(b, g + 2, c - 2, between=piece)
                        else:
                            piece()
                        piece()
                        if c >= 1:
                            weigh_values(b, g, c - 1)
                        piece()
                        if g == G - 1 and c == 6:
                            first_norm(b + 1)
                        if g == G - 1 and c == 8:
                            queries(b + 1)
                    weigh_values(b, g, KC - 1)
                    if g + 1 < G:
                        for u in range(2):
                            max_unit(b, g + 1, u)
                out_unit(b, G - 1)

            def tail(b):
                def heads_transposed():
                    pe.wait_ge(t_free, 1 + b * USES + USES)
                    for h in range(2):
                        for t in range(QT):
                            last = tr(bank[h][:, t * P:(t + 1) * P], attn[:, t, h * P:(h + 1) * P], ident[:, :])
                    last.then_inc(attn_tr, 1)

                def project():
                    pe.wait_ge(attnT_ready, b + 1)
                    for t in range(QT):
                        for k in range(2):
                            last = mm(bank[2 + t // 2][:, (t % 2) * D:(t % 2 + 1) * D],
                                      xnT[:, k, t * P:(t + 1) * P], wp[:, k, :], start=(k == 0), stop=(k == 1))
                    last.then_inc(proj_mm, 1)

                def transpose_x(k):
                    pe.wait_ge(xn_ready, b * 3 + k)
                    for h in range(2):
                        for t in range(QT):
                            last = tr(bank[h][:, t * P:(t + 1) * P], xn[:, t, h * P:(h + 1) * P], ident[:, :])
                    last.then_inc(xnT_mm, 1)

                def ffn_rank():
                    pe.wait_ge(xnT_ready, 1 + b * 3 + 1)
                    for k in range(2):
                        last = mm(bank[2][0:RANK, :], u1[:, k, :], xnT[:, k, :], start=(k == 0), stop=(k == 1))
                    last.then_inc(ffn_mm, 1)

                def ffn(f):
                    if f == 0:
                        pe.wait_ge(ffn_act, b * 2 + 1)
                    if f >= 2:
                        pe.wait_ge(h_act, b * FC + f - 1)
                    if f < FC:
                        mm(bank[f % 2][:, :], v1[:, f * P:(f + 1) * P], pT, start=True, stop=True).then_inc(h_mm, 1)
                    if f >= 2:
                        last = mm(bank[3][0:RANK, :], u2[:, f - 2, :], hT[:, f - 2, :], start=(f == 2),
                                  stop=(f == FC + 1))
                    if f == FC + 1:
                        last.then_inc(ffn_mm, 1)

                def ffn_out():
                    pe.wait_ge(ffn_act, b * 2 + 2)
                    for t in range(QT):
                        last = mm(bank[2 + t // 2][:, (t % 2) * D:(t % 2 + 1) * D], pT[:, t * P:(t + 1) * P],
                                  v2[:, :], start=True, stop=True)
                    last.then_inc(proj_mm, 1)

                def layer_one_queries():
                    pe.wait_ge(xnT_ready, 1 + b * 3 + 2)
                    for k in range(2):
                        last = mm(bank[2][0:A1, :], w1q[:, k, :], xnT[:, k, :], start=(k == 0), stop=(k == 1))
                    last.then_inc(q1_mm, 1)

                def score_stats(t):
                    if t == 0:
                        pe.wait_ge(q1_act, b + 1)
                    for i in range(4):
                        n = 4 * t + i
                        w_ = min(PW, NK - i * PW)
                        if n >= 2:
                            pe.wait_ge(sc_stat, b * 16 + n - 1)
                        mm(bank[i % 2][:, 0:w_], q1T[:, t * P:(t + 1) * P], kv1T[:, i * PW:i * PW + w_],
                           start=True, stop=True).then_inc(sc_mm, 1)

                def queries_to_tokens():
                    for t in range(QT):
                        last = tr(bank[2][:, t * A1:(t + 1) * A1], q1T[0:A1, t * P:(t + 1) * P], ident[0:A1, 0:A1])
                    last.then_inc(q1_tr, 1)

                def scaled_queries():
                    pe.wait_ge(qa_ready, b * 2 + 1)
                    for t in range(QT):
                        last = tr(bank[3][0:R1, t * P:(t + 1) * P], qa[:, t, :], ident[:, :])
                    last.then_inc(q1_tr, 1)

                def layer_one(c):
                    if c == 0:
                        pe.wait_ge(qa_ready, b * 2 + 2)
                    if c < KC:
                        m = key_rows(c)
                        if c >= 2:
                            pe.wait_ge(s1_exp, b * KC + c - 1)
                        mm(bank[c % 2][0:m, :], kv1T[:, c * P:c * P + m], q1a[:, :], start=True,
                           stop=True).then_inc(s1_mm, 1)
                    if c >= 2:
                        e = c - 2
                        m = key_rows(e)
                        pe.wait_ge(s1_exp, b * KC + e + 1)
                        j = e % 4
                        mm(bank[3][32 * j:32 * j + 32, :], v1a[0:m, e, :],
                           probs[0:m, j, (e // 4 % 2) * 512:(e // 4 % 2 + 1) * 512],
                           start=(e < 4), stop=(e + 4 >= KC), skip_group_check=True).then_inc(pv1_mm, 1)

                def layer_one_out():
                    pe.wait_ge(o_copied_1, b + 1)
                    pe.wait_ge(v1_ready, b + 1)
                    for t in range(QT):
                        last = mm(bank[t][:, 0:D + 1], o_sb[:, t * P:(t + 1) * P], wst[:, :], start=True, stop=True)
                    last.then_inc(proj_mm, 1)

                steps = {"attnT": heads_transposed, "proj": project, "x1T": lambda: transpose_x(1), "u1": ffn_rank,
                         "v2": ffn_out, "x2T": lambda: transpose_x(2), "q1": layer_one_queries,
                         "qtr": queries_to_tokens, "qaT": scaled_queries, "out": layer_one_out,
                         "x3T": lambda: transpose_x(3)}
                steps.update({("ffn", f): (lambda f=f: ffn(f)) for f in range(FC + 2)})
                steps.update({("sc", t): (lambda t=t: score_stats(t)) for t in range(QT)})
                steps.update({("s1", c): (lambda c=c: layer_one(c)) for c in range(KC + 2)})
                return steps

            first_norm(0)
            queries(0)
            run_woven(None, head(0))
            attention(0)
            with pe.Fori(1, B) as b:
                run_woven(tail(b - 1), head(b))
                attention(b)
            run_woven(tail(B - 1), None)

        @block.scalar
        def _(act):
            fn = nc.scalar.activation
            act.wait_ge(setup_dve, SETUP_DVE + 1)
            act.wait_ge(setup_pool, 4)
            act.sem_inc(stored, 1)
            def first_norm(b):
                act.wait_ge(ln0_var, b + 1)
                fn(std0[:, :], mv0[:, :, 1], ACT.Sqrt, bias=eps[:, 0:1]).then_inc(ln0_std, 1)

            def queries(b):
                act.wait_ge(q_mm, b + 1)
                fn(kraw[:, KC:KC + 4, :].rearrange("p (n a) d -> p n (a d)", n=2), psum[:, 4:6, :],
                   ACT.Copy).then_inc(q_raw, 1)

            def head(b):
                def context(c):
                    m = key_rows(c)
                    act.wait_ge(kv_mm, b * KC + c + 1)
                    src = bank[6 + c % 2]
                    if c >= 4:
                        act.wait_ge(sq_summed, b * (KC + 1) + c - 3)
                    fn(sq[0:m, c % 4, :], src[0:m, 0:D], ACT.Square)
                    fn(vaug[0:m, c, :, 0:HD], src[0:m, D:2 * D].rearrange("p (h d) -> p h d", h=H), ACT.Copy)
                    fn(kraw[0:m, c, :], src[0:m, 0:D], ACT.Copy).then_inc(kv_raw, 1)

                def norm():
                    act.wait_ge(sq_summed, b * (KC + 1) + KC + 1)
                    fn(rstd[:, :, :], ssq[:, :, :], ACT.Sqrt, bias=eps[:, 0:1], scale=1.0 / HD).then_inc(head_std, 1)

                def first_stack():
                    for u in range(10):
                        stack_evac(b, 0, u)

                def rows(r):
                    for u in range(4 * r, 4 * r + 4):
                        if u % 4 == 3 and u >= 27:
                            stack_evac(b, 1, (u - 27) // 4)

                def first_max():
                    for u in range(2):
                        max_evac(b, 0, u)

                def layer_one_keys():
                    for i in range(4):
                        n = min(PW, NK - i * PW)
                        act.wait_ge(kv1_mm, b * 4 + i + 1)
                        fn(kv1T[0:2 * A1, i * PW:i * PW + n], bank[i % 2][0:2 * A1, 0:n], ACT.Identity,
                           bias=bkv[:, 0:1]).then_inc(kv1_ready, 1)

                steps = {"norm": norm, "stack0": first_stack, "max0": first_max,
                         "kv1": layer_one_keys}
                steps.update({("ctx", c): (lambda c=c: context(c)) for c in range(KC)})
                steps.update({("rows", r): (lambda r=r: rows(r)) for r in range(16)})
                return steps

            tb = bank[6].bitcast(BF16)

            def stack_evac(b, g, u):
                act.wait_ge(t_full, b * USES + USE["stack", g, u] + 1)
                if u < 8:
                    n = 8 * P if u % 2 == 0 else NK - 8 * P
                    dst = kst[g % 3][0:NP, u // 2, (u % 2) * 8 * P:(u % 2) * 8 * P + n]
                else:
                    n = 2 * S
                    dst = qst[g % 3][0:NP, 2 * (u - 8):2 * (u - 8) + 2, :].rearrange("p a q -> p (a q)")
                fn(dst, tb[0:NP, 0:n], ACT.Copy).then_inc(t_free, 1)

            def max_evac(b, g, u):
                act.wait_ge(t_full, b * USES + USE["max", g, u] + 1)
                fn(qst[g % 3][96:NR, 2 * u:2 * u + 2, :].rearrange("p a q -> p (a q)"), tb[96:NR, 0:2 * S],
                   ACT.Copy).then_inc(t_free, 1)

            def attention(b):
                for g in range(G):
                    for c in range(KC):
                        m = key_rows(c)
                        for i in range(2):
                            act.wait_ge(s_full, b * 2 * KC * G + 2 * (KC * g + c) + i + 1)
                            if KC * g + c >= 2:
                                act.wait_ge(pv_mm, b * KC * G + KC * g + c - 1)
                            fn(probs[0:m, (2 * c + i) % 4, :].rearrange("p (a q) -> p a q", a=2),
                               psum[0:m, 2 * i:2 * i + 2, :], ACT.Exp, scale=float(HD) ** 0.5).then_inc(s_exp, 1)
                        if 2 <= c < 12 and g + 2 < G:
                            stack_evac(b, g + 2, c - 2)
                        if g == G - 1 and c == 3:
                            first_norm(b + 1)
                        if g == G - 1 and c == 10:
                            queries(b + 1)
                    act.wait_ge(pv_mm, b * KC * G + KC * (g + 1))
                    if g >= 1:
                        act.wait_ge(t_full, b * USES + USE["out", g - 1, 0] + 1)
                    fn(o_sb[:, :], bank[7], ACT.Copy).then_inc(o_copied, 1)
                    if g + 1 < G:
                        for u in range(2):
                            max_evac(b, g + 1, u)

            def tail(b):
                def layer_norm_std(k):
                    act.wait_ge(ln_var, b * 3 + k)
                    fn(std[:, :], mv[:, :, 1], ACT.Sqrt, bias=eps[:, 0:1]).then_inc(ln_std, 1)

                def ffn_rank():
                    act.wait_ge(ffn_mm, b * 2 + 1)
                    fn(pT, bank[2][0:RANK, :], ACT.Copy).then_inc(ffn_act, 1)

                def ffn(f):
                    if f < FC:
                        act.wait_ge(h_mm, b * FC + f + 1)
                        fn(hT[:, f, :], bank[f % 2], ACT.Gelu_apprx_tanh, bias=b1c[:, f:f + 1]).then_inc(h_act, 1)

                def ffn_out():
                    act.wait_ge(ffn_mm, b * 2 + 2)
                    fn(pT, bank[3][0:RANK, :], ACT.Copy).then_inc(ffn_act, 1)
                    layer_norm_std(2)

                def layer_one_queries():
                    act.wait_ge(q1_mm, b + 1)
                    fn(q1T[0:A1, :], bank[2][0:A1, :], ACT.Identity, bias=bq[:, 0:1], scale=1.0 / A1).then_inc(q1_act, 1)

                def score_std():
                    act.wait_ge(sc_var, b + 1)
                    fn(sg[:, :], mv1[:, :, 1], ACT.Sqrt, scale=NK / (NK - 1.0)).then_inc(sc_std, 1)

                def layer_one(c):
                    if c >= KC:
                        return
                    m = key_rows(c)
                    act.wait_ge(s1_mm, b * KC + c + 1)
                    if c >= 8:
                        act.wait_ge(pv1_mm, b * KC + c - 7)
                    fn(probs[0:m, c % 4, (c // 4 % 2) * 512:(c // 4 % 2 + 1) * 512], bank[c % 2][0:m, :],
                       ACT.Exp, bias=maskcol[0:m, c:c + 1]).then_inc(s1_exp, 1)

                def layer_one_out():
                    act.wait_ge(pv1_mm, b * KC + KC)
                    fn(o_sb[:, :], bank[3], ACT.Copy).then_inc(o_copied_1, 1)
                    layer_norm_std(3)

                def store():
                    act.wait_ge(x_new, b * 3 + 3)
                    act.dma_start(x3_d[b].rearrange("(t p) d -> p t d", p=P), xw[:, :, :]).then_inc(stored, 16)
                    act.wait_ge(xn_ready, b * 3 + 3)
                    act.dma_start(xn_d[b].rearrange("(t p) d -> p t d", p=P), xn[:, :, :]).then_inc(stored, 16)
                    act.wait_ge(xnT_ready, 1 + b * 3 + 3)
                    act.dma_start(xnT_d[b], xnT[:, :, :]).then_inc(stored, 16)

                steps = {"proj": lambda: layer_norm_std(1), "u1": ffn_rank, "v2": ffn_out, "q1": layer_one_queries, "qtr": score_std,
                         "out": layer_one_out, "x3T": store}
                steps.update({("ffn", f): (lambda f=f: ffn(f)) for f in range(FC + 2)})
                steps.update({("s1", c): (lambda c=c: layer_one(c)) for c in range(KC + 2)})
                return steps

            first_norm(0)
            queries(0)
            run_woven(None, head(0))
            attention(0)
            with act.Fori(1, B) as b:
                run_woven(tail(b - 1), head(b))
                attention(b)
            run_woven(tail(B - 1), None)

        @block.vector
        def _(dve):
            v = nc.vector
            steps = [0]

            def setup(ins):
                steps[0] += 1
                ins.then_inc(setup_dve, 1)
                dve.wait_ge(setup_dve, steps[0])

            for i in range(8):
                setup(v.memset(bank[i], 0.0))
            setup(v.memset(vaug[:, :, :, HD:HD + 1], 1.0))
            setup(v.memset(ssq[:, :, :], 1.0))
            setup(v.memset(v1a[:, :, :], 0.0))
            setup(v.memset(v1a[:, :, A1:A1 + 1], 1.0))
            setup(v.memset(kv1T[:, :], 0.0))
            setup(v.memset(kv1T[2 * A1:2 * A1 + 1, :], 1.0))
            setup(v.memset(q1T[:, :], 0.0))
            setup(v.memset(qa[:, :, :], 0.0))
            setup(v.memset(wst[:, :], 0.0))
            setup(v.memset(maskb[:, :, :], 0.0))
            setup(v.memset(mean_w[:, :, :], 0.0))
            dve.wait_ge(weights_in, 16 * NLOAD)
            setup(v.tensor_copy(ctxT[0:B, 0, 0:NK], kraw[0:B, 0:7, :].rearrange("p a b -> p (a b)").bitcast(I32)[:, 0:NK]))
            for k in range(2):
                for n, wt in ((k, wq[:, k, :]), (2 + k, wkv[:, k, 0:D])):
                    wh = wt.rearrange("p (h d) -> p h d", h=H)
                    setup(v.tensor_reduce(mean_w[:, n, :], wh, AX.X, ALU.add))
                    setup(v.tensor_scalar(mean_w[:, n, :], mean_w[:, n, :], 1.0 / HD, None, ALU.mult))
                    setup(v.tensor_tensor(wh, wh, mean_w[:, n, :, None].broadcast_to((P, H, HD)), ALU.subtract))
            for j in range(4):
                setup(v.tensor_reduce(wst[32 * j:32 * j + A1, 0:D],
                                      probs[32 * j:32 * j + A1, :, :].rearrange("p a b -> p (a b)").rearrange(
                                          "p (h n) -> p n h", h=H), AX.X, ALU.add))
            dve.wait_ge(ident_made, 3)
            for j in range(4):
                setup(v.tensor_copy(wst[32 * j:32 * j + 32, D:D + 1],
                                    ident[32 * j:32 * j + 32, 32 * j + A1:32 * j + A1 + 1]))
            setup(v.tensor_scalar(bq[:, :], bq[:, :], 1.0 / A1, None, ALU.mult))
            setup(v.memset(kraw[:, :, :], 0.0))
            assert steps[0] == SETUP_DVE, steps
            dve.wait_ge(setup_pe, 1)
            v.tensor_scalar(maskb[:, 0:KC - 1, :], bank[0][:, 0:(KC - 1) * B].rearrange("p (c b) -> p c b", b=B),
                            -1e-32, None, ALU.mult)
            v.tensor_scalar(maskb[0:KL, KC - 1, :], bank[0][0:KL, (KC - 1) * B:KC * B],
                            -1e-32, None, ALU.mult).then_inc(setup_dve, 1)
            dve.wait_ge(setup_dve, SETUP_DVE + 1)
            dve.sem_inc(t_free, 1)
            dve.sem_inc(xnT_ready, 1)

            def linker(signal, b, steps):
                count = [0]

                def link(ins):
                    count[0] += 1
                    ins.then_inc(signal, 1)
                    dve.wait_ge(signal, b * steps + count[0])
                return link, count

            def layer_norm(src, dst, stats, moments, root, inverse, var, dev, n, ready, link):
                for t in range(QT):
                    ins = v.bn_stats(stats[:, t, :], src[:, t, :])
                link(ins)
                v.tensor_copy(inverse[:, :], stats[:, :, 0])
                for t in range(QT):
                    ins = v.bn_aggr(moments[:, t, :], stats[:, t, :])
                ins.then_inc(var, 1)
                dve.wait_ge(dev, n)
                link(v.reciprocal(inverse[:, :], root[:, :]))
                for t in range(QT):
                    ins = v.tensor_scalar(dst[:, t, :], src[:, t, :], moments[:, t, 0:1], inverse[:, t:t + 1],
                                          ALU.subtract, ALU.mult)
                ins.then_inc(ready, 1)

            def first_norm(b):
                link, count = linker(first_step, b, FIRST_STEPS)
                dve.wait_ge(x_loaded, b * 16 + 16)
                layer_norm(xin, xn0, bst0, mv0, std0, rs0, ln0_var, ln0_std, b + 1, xn0_ready, link)
                dve.wait_ge(xn0T_mm, b + 1)
                v.tensor_copy(xn0T, psum[:, 4:6, :]).then_inc(xn0T_ready, 1)
                assert count[0] == FIRST_STEPS

            def head(b):
                link, count = linker(head_step, b, HEAD_STEPS)

                def context_transposed(c):
                    m = key_rows(c)
                    dve.wait_ge(ctx_tr, b * KC + c + 1)
                    v.tensor_copy(ctxT[:, :, c * P:c * P + m],
                                  bank[4 + c % 2][:, 0:2 * P].rearrange("p (h k) -> p h k", h=2)[:, :, 0:m])\
                        .then_inc(ctxT_ready, 1)

                def context(c):
                    if c + 1 < KC:
                        context_transposed(c + 1)
                    if c >= 1:
                        square_sum(c - 1)

                def square_sum(c):
                    m = key_rows(c)
                    dve.wait_ge(kv_raw, b * KC + c + 1)
                    v.tensor_reduce(ssq[0:m, c, :], sq[0:m, c % 4, :].rearrange("p (h d) -> p h d", h=H),
                                    AX.X, ALU.add).then_inc(sq_summed, 1)

                def norm():
                    square_sum(KC - 1)
                    dve.wait_ge(q_raw, b + 1)
                    dve.wait_ge(sq_summed, b * (KC + 1) + KC)
                    qv = kraw[:, KC:TT, :]
                    link(v.tensor_tensor(sq[:, :, :], qv, qv, ALU.mult))
                    v.tensor_reduce(ssq[:, KC:TT, :], sq[:, :, :].rearrange("p t (h d) -> p t h d", h=H),
                                    AX.X, ALU.add).then_inc(sq_summed, 1)
                    dve.wait_ge(head_std, b + 1)
                    v.reciprocal(rstd[:, :, :], rstd[:, :, :]).then_inc(head_rstd, 1)

                def rows(r):
                    if r == 3:
                        split(b, 1, link)
                    for u in range(4 * r, 4 * r + 4):
                        row_piece(b, 0, u)
                    if r == 15:
                        minus_maximum(b, 0, link)

                def layer_one_values():
                    dve.wait_ge(v1_tr, b + 1)
                    bv = bank[0][:, 0:32 * KC].rearrange("p (c n) -> p c n", n=32)
                    v.tensor_copy(v1a[:, 0:KC - 1, 0:A1], bv[:, 0:KC - 1, A1:2 * A1])
                    v.tensor_copy(v1a[0:KL, KC - 1, 0:A1], bv[0:KL, KC - 1, A1:2 * A1]).then_inc(v1_ready, 1)

                steps = {"ctxT0": lambda: context_transposed(0), "norm": norm, "stack0": lambda: split(b, 0, link),
                         "kv1": layer_one_values}
                steps.update({("ctx", c): (lambda c=c: context(c)) for c in range(KC)})
                steps.update({("rows", r): (lambda r=r: rows(r)) for r in range(16)})
                return steps, count

            def split(b, g, link):
                dve.wait_ge(kf_ready, b * G + g + 1)
                if g >= 2:
                    dve.wait_ge(t_full, b * USES + USE["stack", g - 2, 9] + 1)
                sk = stack[g % 2][:, 0:KC * HG, :].rearrange("p t (s d) -> p t s d", d=HD)
                sqq = stack[g % 2][:, KC * HG:, :].rearrange("p t (s d) -> p t s d", d=HD)
                kfk = kf[:, 0:KC, :].rearrange("p t (h d) -> p (t h) d", d=HD)
                kfq = kf[:, KC:TT, :].rearrange("p t (h d) -> p (t h) d", d=HD)
                NKH, NQH = KC * HG, QT * HG
                v.tensor_copy(sk[:, :, 0:3, :], kfk[:, :, None, :].broadcast_to((P, NKH, 3, HD)))
                v.tensor_copy(sqq[:, :, 3:6:2, :], kfq[:, :, None, :].broadcast_to((P, NQH, 2, HD)))
                link(v.tensor_copy(sqq[:, :, 0, :], kfq))
                v.tensor_tensor(kfk, kfk, sk[:, :, 0, :], ALU.subtract)
                link(v.tensor_tensor(kfq, kfq, sqq[:, :, 0, :], ALU.subtract))
                v.tensor_copy(sk[:, :, 3:5, :], kfk[:, :, None, :].broadcast_to((P, NKH, 2, HD)))
                link(v.tensor_copy(sqq[:, :, 1:5:3, :], kfq[:, :, None, :].broadcast_to((P, NQH, 2, HD))))
                v.tensor_tensor(sk[:, :, 5, :], kfk, sk[:, :, 3, :], ALU.subtract)
                v.tensor_tensor(sqq[:, :, 2, :], kfq, sqq[:, :, 1, :], ALU.subtract).then_inc(stack_ready, 1)

            def row_piece(b, g, u):
                n = 64 * g + u
                dve.wait_ge(m_full, b * 64 * G + n + 1)
                v.tensor_reduce(mx[:, u // 4, u % 4:u % 4 + 1], bank[4 + n % 2][:, 0:PW], AX.X,
                                ALU.max).then_inc(m_free, 1)

            def minus_maximum(b, g, link):
                dve.wait_ge(m_free, b * 64 * G + 64 * (g + 1))
                link(v.tensor_reduce(nmx[:, :], mx[:, :, :], AX.X, ALU.max, negate=True))
                if g >= 1:
                    dve.wait_ge(t_full, b * USES + USE["max", g - 1, 1] + 1)
                link(v.tensor_copy(mxp[:, :, 0], nmx[:, :]))
                link(v.tensor_tensor(mxr[:, :], nmx[:, :], mxp[:, :, 0], ALU.subtract))
                link(v.tensor_copy(mxp[:, :, 1], mxr[:, :]))
                v.tensor_tensor(mxp[:, :, 2], mxr[:, :], mxp[:, :, 1], ALU.subtract).then_inc(mx_ready, 1)

            def attention(b):
                link, count = linker(attention_step, b, ATTENTION_STEPS)

                def heads_out(g):
                    dve.wait_ge(t_full, b * USES + USE["out", g, 0] + 1)
                    o = bank[6].rearrange("p (t n) -> p t n", n=32)
                    link(v.reciprocal(rec[:, :], o[:, :, HD]))
                    for t in range(QT):
                        ins = v.tensor_tensor(
                            attn[:, t, HG * HD * g:HG * HD * (g + 1)].rearrange("p (j d) -> p j d", d=HD),
                            o[:, HG * t:HG * t + HG, 0:HD],
                            rec[:, HG * t:HG * t + HG, None].broadcast_to((P, HG, HD)), ALU.mult)
                    ins.then_inc(t_free, 1)

                for g in range(G):
                    if g + 2 < G:
                        split(b, g + 2, link)
                    if g >= 1:
                        heads_out(g - 1)
                    if g + 1 < G:
                        for u in range(64):
                            row_piece(b, g + 1, u)
                        minus_maximum(b, g + 1, link)
                first_norm(b + 1)
                heads_out(G - 1)
                assert count[0] == ATTENTION_STEPS, count

            def tail(b):
                link, count = linker(tail_step, b, TAIL_STEPS)

                def heads_transposed():
                    dve.wait_ge(attn_tr, b + 1)
                    dve.wait_ge(stored, 1 + b * 48)
                    v.tensor_copy(xnT[:, :, :], psum[:, 0:2, :]).then_inc(attnT_ready, 1)

                def residual_and_norm(dst, k):
                    dve.wait_ge(proj_mm, b * 3 + k)
                    dve.wait_ge(x_based, 1 + b * 3 + k)
                    for i in range(2):
                        half = dst[:, 2 * i:2 * i + 2, :].rearrange("p t d -> p (t d)")
                        ins = v.tensor_tensor(half, bank[2 + i], half, ALU.add)
                    ins.then_inc(x_new, 1)
                    dve.wait_ge(x_new, b * 3 + k)
                    layer_norm(dst, xn, bst, mv, std, rs, ln_var, ln_std, b * 3 + k, xn_ready, link)

                def transposed(k):
                    dve.wait_ge(xnT_mm, b * 3 + k)
                    v.tensor_copy(xnT[:, :, :], psum[:, 0:2, :]).then_inc(xnT_ready, 1)

                def score_stats(t):
                    if t == 0:
                        link(v.tensor_copy(maskcol[:, :, None],
                                           maskb[:, :, b:b + 1] if isinstance(b, int) else maskb[:, :, bass.ds(b, 1)]))
                    for i in range(4):
                        n = 4 * t + i
                        w_ = min(PW, NK - i * PW)
                        dve.wait_ge(sc_mm, b * 16 + n + 1)
                        v.bn_stats(st1[:, t, i, :], bank[i % 2][:, 0:w_]).then_inc(sc_stat, 1)

                def scale_queries():
                    dve.wait_ge(sc_stat, b * 16 + 16)
                    v.tensor_copy(rs[:, :], st1[:, :, 0, 0])
                    for t in range(QT):
                        ins = v.bn_aggr(mv1[:, t, :], st1[:, t, :, :].rearrange("p a b -> p (a b)"))
                    ins.then_inc(sc_var, 1)
                    dve.wait_ge(sc_std, b + 1)
                    link(v.tensor_scalar(rs[:, :], sg[:, :], 1e-8, None, ALU.add))
                    link(v.reciprocal(rs[:, :], rs[:, :]))
                    dve.wait_ge(q1_tr, b * 2 + 1)
                    v.tensor_tensor(qa[:, :, 0:A1], bank[2][:, 0:QT * A1].rearrange("p (t d) -> p t d", d=A1),
                                    rs[:, :, None].broadcast_to((P, QT, A1)), ALU.mult)
                    v.scalar_tensor_tensor(out=qa[:, :, 2 * A1], in0=mv1[:, :, 0], scalar=-1.0, in1=rs[:, :],
                                           op0=ALU.mult, op1=ALU.mult).then_inc(qa_ready, 1)

                def scaled_queries():
                    dve.wait_ge(q1_tr, b * 2 + 2)
                    v.tensor_copy(q1a[:, :], bank[3][0:R1, :]).then_inc(qa_ready, 1)

                def layer_one_out():
                    dve.wait_ge(proj_mm, b * 3 + 3)
                    dve.wait_ge(x_based, 1 + b * 3 + 3)
                    for t in range(QT):
                        ins = v.reciprocal(rs[:, t:t + 1], bank[t][:, D:D + 1])
                    link(ins)
                    for t in range(QT):
                        ins = v.scalar_tensor_tensor(out=xw[:, t, :], in0=bank[t][:, 0:D], scalar=rs[:, t:t + 1],
                                                     in1=xw[:, t, :], op0=ALU.mult, op1=ALU.add)
                    ins.then_inc(x_new, 1)
                    dve.wait_ge(x_new, b * 3 + 3)
                    layer_norm(xw, xn, bst, mv, std, rs, ln_var, ln_std, b * 3 + 3, xn_ready, link)

                steps = {"attnT": heads_transposed, "proj": lambda: residual_and_norm(xw, 1),
                         "x1T": lambda: transposed(1), "v2": lambda: residual_and_norm(xv, 2),
                         "x2T": lambda: transposed(2), "qtr": scale_queries, "qaT": scaled_queries,
                         "out": layer_one_out, "x3T": lambda: transposed(3)}
                steps.update({("sc", t): (lambda t=t: score_stats(t)) for t in range(QT)})
                return steps, count

            def woven(tail_of, head_of):
                t, tc = tail(tail_of) if tail_of is not None else (None, None)
                h, hc = head(head_of) if head_of is not None else (None, None)
                run_woven(t, h)
                assert tc is None or tc[0] == TAIL_STEPS, tc
                assert hc is None or hc[0] == HEAD_STEPS, hc

            first_norm(0)
            woven(None, 0)
            attention(0)
            with dve.Fori(1, B) as b:
                woven(b - 1, b)
                attention(b)
            woven(B - 1, None)


SETUP_DVE = 19 + 1 + 12 + 4 + 4 + 1 + 1
FIRST_STEPS = 2
HEAD_STEPS = 1 + 6 + 4
ATTENTION_STEPS = 2 * 3 + 3 * 4 + G
TAIL_STEPS = 3 * 2 + 1 + 2 + 1


def stage_two(nc, w, x3_d, xn_d, xnT_d, y_d, out, ident, psum):
    phi_d = w["L1_ffn_phi"].rearrange("(k p) n q -> p k (n q)", p=P)
    NC = NS // SC
    with ExitStack() as st:
        sb = lambda name, shape, dt=F32: st.enter_context(nc.sbuf_tensor(name, shape, dt))
        sem = lambda name: st.enter_context(nc.semaphore(name))
        bank = [psum[:, i, :] for i in range(8)]
        negs = sb("negs", [P, B, QT])
        onesr = sb("onesr", [1, P])
        xT = sb("xT", [P, B, 2, S])
        NT = B * NC

        with ExitStack() as s2:
            sb2 = lambda name, shape, dt=F32: s2.enter_context(nc.sbuf_tensor(name, shape, dt))
            sem2 = lambda name: s2.enter_context(nc.semaphore(name))
            disp = sb2("disp", [P, QT, B, SC])
            phi = sb2("phi", [P, 2, SC])
            we = sb2("we", [P, SC // SP_, 2, D])
            be = sb2("be", [P, 2, D])
            bm = sb2("bm", [P, SC])
            bsum = sb2("bsum", [P, SC])
            mxs = sb2("mxs", [P, B])
            xnb = sb2("xnb", [P, 2, QT, D])
            slT = sb2("slT", [P, 2, 2, SC])
            ysb = sb2("ysb", [P, 2, 2, D])
            x_in = sem2("x_in2")
            par_in = sem2("par_in")
            l_mm = sem2("l_mm")
            l_copied = sem2("l_copied")
            first = sem2("first")
            shifted = sem2("shifted")
            exped = sem2("exped")
            summed = sem2("summed")
            normed = sem2("normed")
            dstep = sem2("dstep")
            xn_in = [sem2(f"xn_in{i}") for i in range(2)]
            sl_mm = sem2("sl_mm")
            sl_copied = sem2("sl_copied")
            y_mm = sem2("y_mm")
            y_ready = sem2("y_ready")
            y_stored = [sem2(f"y_stored{i}") for i in range(2)]
            block = s2.enter_context(nc.Block())
            EN = SC // SP_

            @block.sync
            def _(sp):
                for b4 in range(4):
                    sp.dma_start(xT[:, 4 * b4:4 * b4 + 4, :, :],
                                 xnT_d[4 * b4:4 * b4 + 4].rearrange("b p k s -> p b k s")).then_inc(x_in, 16)
                with sp.Fori(0, NC) as s:
                    sp.wait_ge(y_ready, 1 + s * B)
                    sp.dma_start(phi[:, :, :], phi_d[:, :, bass.ds(s * SC, SC)]).then_inc(par_in, 16)
                    sp.dma_start(we[:, :, :, :], w["L1_ffn_W"][bass.ds(s * EN, EN)].rearrange(
                        "n (k p) e -> p n k e", p=P)).then_inc(par_in, 16)
                    for i in range(EN):
                        sp.dma_start(be[32 * (i % 4):32 * (i % 4) + 32, i // 4, :],
                                     w["L1_ffn_b"][bass.ds(s * EN + i, 1), :].broadcast_to((SP_, D)))\
                            .then_inc(par_in, 16)
                    for b in range(B):
                        if b >= 2:
                            sp.wait_ge(sl_mm, 1 + s * B + b - 1)
                        sp.dma_start(xnb[:, b % 2, :, :], xn_d[b].rearrange("(t p) d -> p t d", p=P))\
                            .then_inc(xn_in[b % 2], 16)

            @block.gpsimd
            def _(pool):
                with pool.Fori(0, NC) as s:
                    for t in range(QT):
                        pool.wait_ge(summed, s * QT + t + 1)
                        pool.tensor_tensor(disp[:, t, :, :], disp[:, t, :, :],
                                           bsum[:, None, :].broadcast_to((P, B, SC)), ALU.mult).then_inc(normed, 1)

            @block.tensor
            def _(pe):
                mm = nc.tensor.matmul
                pe.wait_ge(x_in, 64)
                pe.sem_inc(sl_mm, 1)
                with pe.Fori(0, NC) as s:
                    pe.wait_ge(par_in, (s + 1) * 16 * (2 + EN))
                    for t in range(QT):
                        for bb in range(B // 2):
                            n = t * B // 2 + bb
                            if n >= 4:
                                pe.wait_ge(l_copied, s * QT * B // 2 + n - 3)
                            for a in range(2):
                                for k in range(2):
                                    last = mm(bank[n % 4][:, a * SC:(a + 1) * SC],
                                              xT[:, 2 * bb + a, k, t * P:(t + 1) * P], phi[:, k, :],
                                              start=(k == 0), stop=(k == 1))
                            last.then_inc(l_mm, 1)
                    pe.wait_ge(normed, s * QT + QT)

                    def slots(b):
                        pe.wait_ge(xn_in[b % 2], (s * (B // 2) + b // 2 + 1) * 16)
                        if b >= 1:
                            pe.wait_ge(sl_copied, s * B + b)
                        for h in range(2):
                            for t in range(QT):
                                last = mm(bank[4 + h][:, 0:SC], xnb[:, b % 2, t, h * P:(h + 1) * P],
                                          disp[:, t, b, :], start=(t == 0), stop=(t == QT - 1))
                        last.then_inc(sl_mm, 1)

                    def experts(b):
                        pe.wait_ge(sl_copied, s * B + b + 1)
                        if b >= 1:
                            pe.wait_ge(y_ready, 1 + s * B + b)
                        for a in range(SC // P):
                            for k in range(2):
                                for j in range(4):
                                    c0 = a * P + 32 * j
                                    last = mm(bank[6 + a][32 * j:32 * j + 32, 0:D], slT[:, b % 2, k, c0:c0 + 32],
                                              we[:, 4 * a + j, k, :], start=(k == 0), stop=(k == 1),
                                              skip_group_check=True)
                        last.then_inc(y_mm, 1)

                    slots(0)
                    for b in range(B):
                        if b + 1 < B:
                            slots(b + 1)
                        experts(b)

            @block.scalar
            def _(act):
                fn = nc.scalar.activation
                for i in range(2):
                    act.sem_inc(y_stored[i], 1)
                with act.Fori(0, NC) as s:
                    def store_y(b):
                        act.wait_ge(y_ready, 1 + s * B + b + 1)
                        act.dma_start(y_d[b, bass.ds(s * SC, SC), :].rearrange("(a p) e -> p a e", p=P),
                                      ysb[:, b % 2, :, :]).then_inc(y_stored[b % 2], 16)

                    act.wait_ge(sl_mm, 1 + s * B)
                    for t in range(QT):
                        for bb in range(B // 2):
                            n = t * B // 2 + bb
                            act.wait_ge(l_mm, s * QT * B // 2 + n + 1)
                            fn(disp[:, t, 2 * bb:2 * bb + 2, :].rearrange("p a n -> p (a n)"), bank[n % 4],
                               ACT.Copy).then_inc(l_copied, 1)
                        if t >= 1:
                            act.wait_ge(shifted, s * QT + t)
                            fn(disp[:, t - 1, :, :], disp[:, t - 1, :, :], ACT.Exp).then_inc(exped, 1)
                    act.wait_ge(shifted, s * QT + QT)
                    fn(disp[:, QT - 1, :, :], disp[:, QT - 1, :, :], ACT.Exp).then_inc(exped, 1)
                    for b in range(B):
                        act.wait_ge(sl_mm, 1 + s * B + b + 1)
                        if b >= 2:
                            act.wait_ge(y_mm, s * B + b - 1)
                        for h in range(2):
                            e = fn(slT[:, b % 2, h, :], bank[4 + h][:, 0:SC], ACT.Copy)
                        e.then_inc(sl_copied, 1)
                        if b >= 1:
                            store_y(b - 1)
                    store_y(B - 1)
                for i in range(2):
                    act.wait_ge(y_stored[i], 1 + 16 * NT // 2)

            @block.vector
            def _(dve):
                v = nc.vector
                v.memset(onesr[:, :], 1.0)
                v.memset(negs[:, :, :], -3.0e38).then_inc(first, 1)
                dve.wait_ge(first, 1)
                dve.sem_inc(y_ready, 1)
                PER = QT * 3
                with dve.Fori(0, NC) as s:
                    count = [0]

                    def link(ins):
                        count[0] += 1
                        ins.then_inc(dstep, 1)
                        dve.wait_ge(dstep, s * PER + count[0])

                    def shift(t):
                        dve.wait_ge(l_copied, s * QT * B // 2 + (t + 1) * B // 2)
                        v.tensor_reduce(mxs[:, :], disp[:, t, :, :], AX.X, ALU.max)
                        link(v.tensor_reduce(bm[:, :], disp[:, t, :, :].rearrange("p b n -> p n b"), AX.X, ALU.max))
                        v.tensor_tensor(disp[:, t, :, :], disp[:, t, :, :],
                                        bm[:, None, :].broadcast_to((P, B, SC)), ALU.subtract).then_inc(shifted, 1)
                        link(v.tensor_tensor(negs[:, :, t], negs[:, :, t], mxs[:, :], ALU.max))

                    def total(t):
                        dve.wait_ge(exped, s * QT + t + 1)
                        if t >= 1:
                            dve.wait_ge(normed, s * QT + t)
                        link(v.tensor_reduce(bsum[:, :], disp[:, t, :, :].rearrange("p b n -> p n b"), AX.X, ALU.add))
                        v.reciprocal(bsum[:, :], bsum[:, :]).then_inc(summed, 1)

                    shift(0)
                    for t in range(QT):
                        if t + 1 < QT:
                            shift(t + 1)
                        total(t)
                    for b in range(B):
                        dve.wait_ge(y_mm, s * B + b + 1)
                        dve.wait_ge(y_stored[b % 2], 1 + (s * (B // 2) + b // 2) * 16)
                        for a in range(2):
                            ins = v.tensor_tensor(ysb[:, b % 2, a, :], bank[6 + a][:, 0:D], be[:, a, :], ALU.add)
                        ins.then_inc(y_ready, 1)
                    assert count[0] == PER

        with ExitStack() as s3:
            sb3 = lambda name, shape, dt=F32: s3.enter_context(nc.sbuf_tensor(name, shape, dt))
            sem3 = lambda name: s3.enter_context(nc.semaphore(name))
            KS = NS // P
            phi = sb3("phi_all", [P, 2, NS])
            ya = sb3("ya", [P, KS, D + 1])
            x3 = sb3("x3", [P, QT, D])
            xc = sb3("xc", [P, 2, S])
            ng = sb3("ng", [P, QT])
            ngr = sb3("ngr", [1, S])
            ex = sb3("ex", [P, 3, S])
            rc = sb3("rc", [P, QT])
            par = sem3("par3")
            y_in = sem3("y_in")
            x_in = sem3("x_in3")
            made = sem3("made3")
            n_ready = sem3("n_ready")
            n_tr = sem3("n_tr")
            nr_ready = sem3("nr_ready")
            c_mm = sem3("c_mm")
            c_exp = sem3("c_exp")
            o_mm = sem3("o_mm")
            o_rc = sem3("o_rc")
            o_ready = sem3("o_ready")
            o_stored = sem3("o_stored")
            block = s3.enter_context(nc.Block())

            @block.sync
            def _(sp):
                sp.dma_start(phi[:, :, :], phi_d).then_inc(par, 16)
                sp.sem_inc(o_stored, 1)
                with sp.Fori(0, B) as b:
                    sp.wait_ge(o_mm, 1 + b * KS)
                    sp.dma_start(ya[:, :, 0:D], y_d[b].rearrange("(c p) e -> p c e", p=P)).then_inc(y_in, 16)
                    sp.wait_ge(o_stored, 1 + b * 16)
                    sp.dma_start(x3[:, :, :], x3_d[b].rearrange("(t p) d -> p t d", p=P)).then_inc(x_in, 16)
                    sp.wait_ge(o_ready, 1 + b + 1)
                    sp.dma_start(out[b].rearrange("(t p) d -> p t d", p=P), x3[:, :, :]).then_inc(o_stored, 16)
                sp.wait_ge(o_stored, 1 + 16 * B)

            @block.tensor
            def _(pe):
                mm = nc.tensor.matmul
                pe.wait_ge(par, 16)
                pe.wait_ge(made, 1)
                pe.sem_inc(o_mm, 1)
                with pe.Fori(0, B) as b:
                    pe.wait_ge(n_ready, b + 1)
                    for t in range(QT):
                        last = nc.tensor.transpose(bank[0][0:1, t * P:(t + 1) * P], ng[:, t:t + 1], ident[:, :])
                    last.then_inc(n_tr, 1)
                    pe.wait_ge(nr_ready, b + 1)
                    for c in range(KS + 2):
                        if c < KS:
                            if c >= 4:
                                pe.wait_ge(c_exp, b * KS + c - 3)
                            o = bank[c % 4]
                            for k in range(2):
                                mm(o, phi[:, k, c * P:(c + 1) * P], xc[:, k, :], start=(k == 0), stop=False)
                            mm(o, onesr[:, :], ngr[:, :], start=False, stop=True).then_inc(c_mm, 1)
                        if c >= 2:
                            e = c - 2
                            if e == 0:
                                pe.wait_ge(y_in, b * 16 + 16)
                                pe.wait_ge(o_ready, 1 + b)
                            pe.wait_ge(c_exp, b * KS + e + 1)
                            for t in range(QT):
                                last = mm(bank[4 + t][:, 0:D + 1], ex[:, e % 3, t * P:(t + 1) * P], ya[:, e, :],
                                          start=(e == 0), stop=(e == KS - 1))
                            last.then_inc(o_mm, 1)

            @block.scalar
            def _(act):
                with act.Fori(0, B) as b:
                    for c in range(KS):
                        act.wait_ge(c_mm, b * KS + c + 1)
                        if c >= 3:
                            act.wait_ge(o_mm, 1 + b * KS + c - 2)
                        nc.scalar.activation(ex[:, c % 3, :], bank[c % 4], ACT.Exp).then_inc(c_exp, 1)

            @block.vector
            def _(dve):
                v = nc.vector
                v.memset(ya[:, :, D:D + 1], 1.0).then_inc(made, 1)
                dve.sem_inc(o_ready, 1)
                with dve.Fori(0, B) as b:
                    v.tensor_scalar(ng[:, :, None], negs[:, bass.ds(b, 1), :].rearrange("p a t -> p t a"), -1.0, None,
                                    ALU.mult).then_inc(n_ready, 1)
                    v.tensor_copy(xc[:, :, :], xT[:, bass.ds(b, 1), :, :].rearrange("p a k s -> p (a k) s"))
                    dve.wait_ge(n_tr, b + 1)
                    v.tensor_copy(ngr[:, :], bank[0][0:1, :]).then_inc(nr_ready, 1)
                    dve.wait_ge(o_mm, 1 + b * KS + KS)
                    dve.wait_ge(x_in, b * 16 + 16)
                    for t in range(QT):
                        ins = v.reciprocal(rc[:, t:t + 1], bank[4 + t][:, D:D + 1])
                    ins.then_inc(o_rc, 1)
                    dve.wait_ge(o_rc, b + 1)
                    for t in range(QT):
                        ins = v.scalar_tensor_tensor(out=x3[:, t, :], in0=bank[4 + t][:, 0:D], scalar=rc[:, t:t + 1],
                                                     in1=x3[:, t, :], op0=ALU.mult, op1=ALU.add)
                    ins.then_inc(o_ready, 1)


_INS = ['x', 'ctx_1024', 'mask_BxS2_bk0', 'L0_xattn_Wq', 'L0_xattn_Wkv', 'L0_xattn_Wp', 'L0_xattn_bp',
        'L0_xattn_ln_g', 'L0_xattn_ln_b', 'L0_ffn_U1', 'L0_ffn_V1', 'L0_ffn_b1', 'L0_ffn_U2', 'L0_ffn_V2',
        'L0_ffn_b2', 'L1_xattn_Wq', 'L1_xattn_bq', 'L1_xattn_Wk', 'L1_xattn_bk', 'L1_xattn_Wv', 'L1_xattn_bv',
        'L1_xattn_Wout', 'L1_xattn_bout', 'L1_ffn_phi', 'L1_ffn_W', 'L1_ffn_b']


def kernel(**inputs):
    import numpy as _np
    import concourse.bacc as _bacc
    from concourse import mybir as _mybir
    from concourse.bass_utils import run_bass_kernel_spmd as _run

    nc = _bacc.Bacc("TRN2", target_bir_lowering=False, num_devices=1)
    arrays, args = {}, {}
    for name in _INS:
        a = _np.ascontiguousarray(inputs[name])
        if a.dtype.kind == "b":
            a = a.astype(_np.int32)
        arrays[f"in_{name}"] = a
        args[name] = nc.dram_tensor(f"in_{name}", a.shape, _mybir.dt.from_np(a.dtype), kind="ExternalInput").ap()
    out = nc.dram_tensor("out_0", (B, S, D), F32, kind="ExternalOutput").ap()
    x3_d = nc.dram_tensor("x3_scratch", (B, S, D), F32, kind="Internal").ap()
    xn_d = nc.dram_tensor("xn_scratch", (B, S, D), F32, kind="Internal").ap()
    xnT_d = nc.dram_tensor("xnT_scratch", (B, P, 2, S), F32, kind="Internal").ap()
    y_d = nc.dram_tensor("y_scratch", (B, NS, D), F32, kind="Internal").ap()
    layers(nc, args["x"], args["ctx_1024"], args["mask_BxS2_bk0"], args, x3_d, xn_d, xnT_d, y_d, out)
    r = _run(nc, [arrays], core_ids=[0])
    return r.results[0]["out_0"]
```
